# Optimizing a Trainium2 kernel written in Bass

```python
import numpy as np
import jax
import jax.numpy as jnp

def _softmax(x, axis=-1):
    return jax.nn.softmax(x, axis=axis)

def _gelu(x):
    return jax.nn.gelu(x, approximate=True)

def _silu(x):
    return jax.nn.silu(x)

def _sigmoid(x):
    return jax.nn.sigmoid(x)

def _layernorm(x, axis=-1, eps=1e-05):
    m = jnp.mean(x, axis=axis, keepdims=True)
    v = jnp.var(x, axis=axis, keepdims=True)
    return (x - m) / jnp.sqrt(v + eps)

def _scatter_add(tgt, idx, src, axis=0):
    return tgt.at[idx].add(src)

def _segment_sum(src, seg, n):
    return jax.ops.segment_sum(src, seg, n)
kernel_name = 'mk_xattn_seq_d1_seqx_r8_0a319d'

def setup_inputs(seed: int=0):
    np.random.seed(seed)
    _w = jnp.asarray

    def _rec_inputs():
        import jax
        import jax.numpy as jnp
        _rk = jax.random.key(seed)
        x = -0.0002928 + 1 * jax.random.normal(jax.random.fold_in(_rk, 1), (128, 64, 128), jnp.float32)
        _lenS = 64 - jax.random.randint(jax.random.fold_in(_rk, 7), (128,), 0, max(1, 64 // 4) + 1, jnp.int32)
        _lenS2 = 64 - jax.random.randint(jax.random.fold_in(_rk, 8), (128,), 0, max(1, 64 // 4) + 1, jnp.int32)
        _ctx_1024P = jax.random.normal(jax.random.fold_in(_rk, 11), (128, 16, 128), jnp.float32)
        _ctx_1024c = jax.random.dirichlet(jax.random.fold_in(_rk, 511), 0.3 * jnp.ones((16,), jnp.float32), (128, 64))
        _ctx_1024t = jnp.einsum('bsk,bkd->bsd', _ctx_1024c, _ctx_1024P)
        _ctx_1024t = _ctx_1024t * jax.lax.rsqrt(jnp.mean(jnp.square(_ctx_1024t)) + 1e-12) * 0.953939
        ctx_1024 = -1.39393e-06 + 0.999914 * (_ctx_1024t + 0.3 * jax.random.normal(jax.random.fold_in(_rk, 611), (128, 64, 128), jnp.float32))
        return (x, ctx_1024)
    x, ctx_1024 = _rec_inputs()

    def _L0_xattn_setup():
        import jax, jax.numpy as jnp
        import numpy as np
        DIM = 128
        HEADS = 16
        HEAD_DIM = DIM // HEADS
        SCALE = HEAD_DIM ** (-0.5)
        EPS = 1e-05
        key = jax.random.key(seed)
        ks = jax.random.split(key, 12)
        b, n, d = (2, 256, DIM)
        s = d ** (-0.5)
        return {'x': jax.random.normal(ks[0], (b, n, d), jnp.float32), 'context': jax.random.normal(ks[1], (b, n, d), jnp.float32), 'Wq': jax.random.normal(ks[2], (d, d), jnp.float32) * s, 'bq': jnp.zeros((d,), jnp.float32), 'Wk': jax.random.normal(ks[3], (d, d), jnp.float32) * s, 'bk': jnp.zeros((d,), jnp.float32), 'Wv': jax.random.normal(ks[4], (d, d), jnp.float32) * s, 'bv': jnp.zeros((d,), jnp.float32), 'Wo': jax.random.normal(ks[5], (d, d), jnp.float32) * s, 'bo': jnp.zeros((d,), jnp.float32), 'gamma': jnp.ones((d,), jnp.float32), 'beta': jnp.zeros((d,), jnp.float32)}
    _L0_xattn_all = _L0_xattn_setup()
    _L0_xattn_in = {k: v for k, v in _L0_xattn_all.items() if k in ('Wq', 'bq', 'Wk', 'bk', 'Wv', 'bv', 'Wo', 'bo', 'gamma', 'beta')}
    del _L0_xattn_all
    return {'x': x, 'ctx_1024': ctx_1024, 'L0_xattn_Wq': _L0_xattn_in['Wq'], 'L0_xattn_bq': _L0_xattn_in['bq'], 'L0_xattn_Wk': _L0_xattn_in['Wk'], 'L0_xattn_bk': _L0_xattn_in['bk'], 'L0_xattn_Wv': _L0_xattn_in['Wv'], 'L0_xattn_bv': _L0_xattn_in['bv'], 'L0_xattn_Wo': _L0_xattn_in['Wo'], 'L0_xattn_bo': _L0_xattn_in['bo'], 'L0_xattn_gamma': _L0_xattn_in['gamma'], 'L0_xattn_beta': _L0_xattn_in['beta']}

def reference(x, ctx_1024, L0_xattn_Wq, L0_xattn_bq, L0_xattn_Wk, L0_xattn_bk, L0_xattn_Wv, L0_xattn_bv, L0_xattn_Wo, L0_xattn_bo, L0_xattn_gamma, L0_xattn_beta):
    import jax
    import jax.numpy as jnp

    def _L0_xattn_ref(x, context, Wq, bq, Wk, bk, Wv, bv, Wo, bo, gamma, beta):
        import jax, jax.numpy as jnp
        import numpy as np
        DIM = 128
        HEADS = 16
        HEAD_DIM = DIM // HEADS
        SCALE = HEAD_DIM ** (-0.5)
        EPS = 1e-05
        b, n, d = x.shape
        h, hd = (HEADS, HEAD_DIM)
        q = (x @ Wq + bq).reshape(b, n, h, hd).transpose(0, 2, 1, 3)
        k = (context @ Wk + bk).reshape(b, n, h, hd).transpose(0, 2, 1, 3)
        v = (context @ Wv + bv).reshape(b, n, h, hd).transpose(0, 2, 1, 3)
        dots = jnp.einsum('bhqd,bhkd->bhqk', q, k) * SCALE
        attn = jax.nn.softmax(dots, axis=-1)
        out = jnp.einsum('bhqk,bhkd->bhqd', attn, v)
        out = out.transpose(0, 2, 1, 3).reshape(b, n, d)
        out = out @ Wo + bo
        y = out + x
        mu = jnp.mean(y, axis=-1, keepdims=True)
        var = jnp.mean((y - mu) ** 2, axis=-1, keepdims=True)
        return (y - mu) * jax.lax.rsqrt(var + EPS) * gamma + beta
    x = _L0_xattn_ref(x, ctx_1024, L0_xattn_Wq, L0_xattn_bq, L0_xattn_Wk, L0_xattn_bk, L0_xattn_Wv, L0_xattn_bv, L0_xattn_Wo, L0_xattn_bo, L0_xattn_gamma, L0_xattn_beta)
    return x

_drawn_inputs = setup_inputs


def setup_inputs(seed=0):
    import zlib

    import numpy as np

    out = dict(_drawn_inputs(seed))
    spreads = {'L0_xattn_bq': (0.0, 0.327),
     'L0_xattn_bk': (0.0, 0.8),
     'L0_xattn_bv': (0.0, 0.1),
     'L0_xattn_bo': (0.0, 0.1),
     'L0_xattn_gamma': (1.0, 0.2),
     'L0_xattn_beta': (0.0, 0.1)}
    factors = {}
    for name, (base, spread) in spreads.items():
        noise = np.random.default_rng([zlib.crc32(name.encode()), seed]).standard_normal(out[name].shape)
        drawn = base * np.exp(spread * noise) if base else spread * noise
        out[name] = jnp.asarray(drawn.astype(out[name].dtype))
    for name, factor in factors.items():
        out[name] = (out[name] * factor).astype(out[name].dtype)
    return out
```

```python
from contextlib import ExitStack

import concourse.bass as bass
from concourse import mybir

F32 = mybir.dt.float32
BF16 = mybir.dt.bfloat16
ALU = mybir.AluOpType
ACT = mybir.ActivationFunctionType
AX_X = mybir.AxisListType.X

P = 128
BATCHES = 128
SEQ = 64
HEADS = 16
HD = P // HEADS
PAIRS = HEADS // 2
EPS = 1e-5
SCALE = HD ** -0.5

CB = 8
T = CB * SEQ
CHUNKS = BATCHES // CB
TILES = T // P
RING = 3
PARTS = 3
RUNS = [(0, 3), (3, 2), (5, 1)]
PRODUCTS = 6
MEMBER_ROWS = PRODUCTS * HD
STACK = 2 * MEMBER_ROWS
MAX_ROWS = 2 * PARTS
FULL = STACK + MAX_ROWS
UNITS = CB
HALF = PAIRS // 2


class Chunk:

    def __init__(self, turn, base):
        self.turn, self.base = turn, base
        self.ring = base % RING

    def next(self, n):
        return Chunk(self.turn, self.base + n)

    def exists(self):
        return not isinstance(self.turn, int) or 0 <= self.base < CHUNKS

    def has(self, back):
        return self.next(-back).exists()

    def times(self, per, plus=0):
        return self.turn * (per * RING) + (per * self.base + plus)

    def ring_times(self, per, plus=0):
        return self.turn * per + (per * (self.base // RING) + plus)


def if_exists(c, do, *args):
    if c.exists():
        do(c, *args)


def slots(eng, slot):
    first = RING + 1
    full = (CHUNKS - RING - first) // RING
    for n in range(-2, first):
        slot(Chunk(0, n))
    with eng.Fori(0, full) as turn:
        for r in range(RING):
            slot(Chunk(turn, first + r))
    for n in range(first + full * RING, CHUNKS + 1):
        slot(Chunk(0, n))


def xattn_program(nc, xT, cT, x, wq, wk, wv, wo, bqk, bo, bv_cols, gamma, beta, ident, den_mask,
                  max_ones, out):
    x_v = x.rearrange("(c t p) d -> p c t d", p=P, t=TILES)
    out_v = out.rearrange("(c t p) d -> p c t d", p=P, t=TILES)

    with ExitStack() as ctx:
        def sb(name, shape, dt=F32):
            return ctx.enter_context(nc.sbuf_tensor(name, shape, dt))

        def bank(name, dt=F32):
            return ctx.enter_context(nc.psum_tensor(name, [P, 512 if dt == F32 else 1024], dt))

        def sem(name):
            return ctx.enter_context(nc.semaphore(name))

        wq_s, wk_s, wv_s, wo_s = (sb(n, [P, P]) for n in ("wq_s", "wk_s", "wv_s", "wo_s"))
        bqk_s = sb("bqk_s", [P, 2])
        bv_s = sb("bv_s", [P, P])
        bo_s = sb("bo_s", [P, P])
        gamma_s = sb("gamma_s", [P, P])
        beta_s = sb("beta_s", [P, P])
        ident_s = sb("ident_s", [P, P], BF16)
        den_mask_s = sb("den_mask_s", [P, 2, 32])
        xT_s = sb("xT_s", [P, RING, T])
        cT_s = sb("cT_s", [P, RING, T])
        x_s = sb("x_s", [P, RING, TILES, P])
        o_s = sb("o_s", [P, RING, TILES, P])
        parts = [[sb(f"part{i}{t}", [P, T], BF16) for t in range(PARTS)] for i in range(2)]
        rest = [sb(f"rest{i}", [P, T]) for i in range(2)]
        q_stack = [sb(f"q_stack{r}", [P, PAIRS, T], BF16) for r in range(RING)]
        k_stack = [sb(f"k_stack{r}", [P, PAIRS, CB, 2, SEQ], BF16) for r in range(RING)]
        v_cols = [sb(f"v_cols{r}", [P, CB, PAIRS, 32]) for r in range(RING)]
        probs = sb("probs", [P, PAIRS, CB, SEQ])
        neg_max = sb("neg_max", [P, CB // 2, PAIRS, 2])
        max_rest = sb("max_rest", [P, CB // 2, PAIRS, 2])
        max_parts = sb("max_parts", [P, CB // 2, PAIRS, 2, PARTS], BF16)
        maxT = sb("maxT", [P, 2, P], BF16)
        recip = sb("recip", [P, T])
        attnT = sb("attnT", [P, T])
        stats = sb("stats", [P, TILES, 6])
        minus_half, quarter = sb("minus_half", [P, TILES]), sb("quarter", [P, TILES])
        mean_sum = sb("mean_sum", [P, TILES])
        mean_diff = sb("mean_diff", [P, TILES])
        dev_sum = sb("dev_sum", [P, TILES])
        diff_sq = sb("diff_sq", [P, TILES])
        neg_mean = sb("neg_mean", [P, TILES])
        scaled_dev = sb("scaled_dev", [P, TILES])
        var4 = sb("var4", [P, TILES])
        var_eps = sb("var_eps", [P, TILES])
        rstd = sb("rstd", [P, TILES])
        shift = sb("shift", [P, TILES])

        row_banks = [bank(f"row_bank{i}") for i in range(2)]
        key_banks = [bank(f"key_bank{i}") for i in range(2)]
        pv_bank = bank("pv_bank")
        den_bank = bank("den_bank")
        misc0 = bank("misc0")
        misc1 = bank("misc1")

        part_dram = nc.dram_tensor("part_dram", [RING, 2, PARTS, HD, 2, PAIRS, T], BF16, kind="Internal").ap()
        max_dram = nc.dram_tensor("max_dram", [PAIRS, MAX_ROWS, CB // 2, P], BF16, kind="Internal").ap()

        consts_loaded = sem("consts_loaded")
        ones_loaded = sem("ones_loaded")
        stack_zeroed = sem("stack_zeroed")
        v_zeroed = sem("v_zeroed")
        half_set = sem("half_set")
        bias_product = sem("bias_product")
        bias_ready = sem("bias_ready")
        xT_loaded = [sem(f"xT_loaded{r}") for r in range(RING)]
        cT_loaded = [sem(f"cT_loaded{r}") for r in range(RING)]
        x_loaded = [sem(f"x_loaded{r}") for r in range(RING)]
        projected = [sem("q_projected"), sem("k_projected")]
        v_projected = sem("v_projected")
        hi_ready = [sem("q_hi_ready"), sem("k_hi_ready")]
        rest_ready = [sem("q_rest_ready"), sem("k_rest_ready")]
        mid_ready = [sem("q_mid_ready"), sem("k_mid_ready")]
        lo_ready = [sem("q_lo_ready"), sem("k_lo_ready")]
        parts_written = [sem("q_parts_written"), sem("k_parts_written")]
        stack_loaded = [sem(f"stack_loaded{r}") for r in range(RING)]
        v_placed = sem("v_placed")
        rows_scored = sem("rows_scored")
        rows_maxed = sem("rows_maxed")
        max_step = sem("max_step")
        max_split = sem("max_split")
        max_turned = sem("max_turned")
        maxT_ready = sem("maxT_ready")
        maxT_written = sem("maxT_written")
        max_loaded = [sem(f"max_loaded{r}") for r in range(RING)]
        keys_scored = sem("keys_scored")
        exp_done = sem("exp_done")
        pv_done = sem("pv_done")
        den_done = sem("den_done")
        recip_done = sem("recip_done")
        attn_ready = sem("attn_ready")
        out_projected = sem("out_projected")
        x_biased = sem("x_biased")
        y_ready = sem("y_ready")
        moments_ready = sem("moments_ready")
        norm_step = sem("norm_step")
        norm_ready = sem("norm_ready")
        normed = sem("normed")
        scaled = sem("scaled")
        out_ready = sem("out_ready")
        stored = [sem(f"stored{r}") for r in range(RING)]

        const_loads = [(wq_s, wq), (wk_s, wk), (bqk_s, bqk), (wv_s, wv), (ident_s, ident),
                       (wo_s, wo), (bv_s, bv_cols), (bo_s, bo), (gamma_s, gamma), (beta_s, beta)]
        CONSTS = 16 * (len(const_loads) + 1)

        block = ctx.enter_context(nc.Block())

        @block.sync
        def _(sp):
            def load_turned(c):
                if c.has(RING):
                    sp.wait_ge(projected[0], c.times(1, 1 - RING))
                sp.dma_start(xT_s[:, c.ring, :], xT[:, bass.ds(c.times(T), T)]).then_inc(xT_loaded[c.ring], 16)
                if c.has(RING):
                    sp.wait_ge(v_projected, c.times(2, 2 * (1 - RING)))
                sp.dma_start(cT_s[:, c.ring, :], cT[:, bass.ds(c.times(T), T)]).then_inc(cT_loaded[c.ring], 16)

            def load_x(c):
                if c.has(RING):
                    sp.wait_ge(normed, c.times(1, 1 - RING))
                sp.dma_start(x_s[:, c.ring, :, :], x_v[:, c.times(1), :, :]).then_inc(x_loaded[c.ring], 16)

            def write_parts(c, i):
                for t, ready in enumerate((hi_ready, mid_ready, lo_ready)):
                    sp.wait_ge(ready[i], c.times(1, 1))
                    at = t if i == 0 else PARTS - 1 - t
                    sp.dma_start(part_dram[c.ring, i, at].rearrange("d e hp x -> (e hp) d x"),
                                 parts[i][t][:, :]).then_inc(parts_written[i], 16)

            def load_stack(c, i):
                sp.wait_ge(parts_written[i], c.times(16 * PARTS, 16 * PARTS))
                if not isinstance(c.turn, int) or c.base < RING:
                    sp.wait_ge(stack_zeroed, RING)
                rows_dram = part_dram[c.ring, i].rearrange("t d e hp x -> e (t d) (hp x)")
                for e in range(2):
                    for first, n in RUNS:
                        row = e * MEMBER_ROWS + first * HD
                        at = 0 if i == 0 else (PARTS - n) * HD
                        src = rows_dram[e, at:at + n * HD, :]
                        if i == 0:
                            dst = q_stack[c.ring][row:row + n * HD, :, :].rearrange("r hp x -> r (hp x)")
                        else:
                            dst = k_stack[c.ring][row:row + n * HD, :, :, e, :].rearrange("r hp b s -> r (hp b) s")
                            src = src.rearrange("r (hb s) -> r hb s", s=SEQ)
                        sp.dma_start(dst, src).then_inc(stack_loaded[c.ring], 16)

            def move_max(c):
                sp.wait_ge(maxT_ready, c.times(1, 1))
                rows = max_dram.rearrange("hp r b x -> (hp r) b x")
                for b in range(CB // 2):
                    p0 = (b % 2) * PAIRS * MAX_ROWS
                    sp.dma_start(rows[:, b, :], maxT[p0:p0 + PAIRS * MAX_ROWS, b // 2, :]).then_inc(maxT_written, 16)
                sp.wait_ge(maxT_written, c.times(16 * CB // 2, 16 * CB // 2))
                sp.dma_start(q_stack[c.ring][STACK:FULL, :, :],
                             max_dram.rearrange("hp r b x -> r hp (b x)")).then_inc(max_loaded[c.ring], 16)

            def store(c):
                sp.wait_ge(out_ready, c.times(1, 1))
                sp.dma_start(out_v[:, c.times(1), :, :], o_s[:, c.ring, :, :]).then_inc(stored[c.ring], 16)

            sp.dma_start(*[a[:] for a in const_loads[0]]).then_inc(consts_loaded, 16)
            load_turned(Chunk(0, 0))
            for dst, src in const_loads[1:]:
                sp.dma_start(dst[:], src[:]).then_inc(consts_loaded, 16)
            sp.dma_start(den_mask_s[:, :, :], den_mask[:]).then_inc(consts_loaded, 16)
            for r in range(RING):
                sp.wait_ge(stack_zeroed, r + 1)
                sp.dma_start(k_stack[r][STACK:FULL, :, :, :, :].rearrange("r hp b e s -> r (hp b e s)"),
                             max_ones[:]).then_inc(ones_loaded, 16)

            def slot(n):
                for c, do in ((n.next(3), load_turned), (n.next(1), load_x)):
                    if c.exists():
                        do(c)
                c = n.next(2)
                if c.exists():
                    write_parts(c, 0)
                    write_parts(c, 1)
                    load_stack(c, 0)
                    load_stack(c, 1)
                if n.next(1).exists():
                    move_max(n.next(1))
                if n.next(-1).exists():
                    store(n.next(-1))

            slots(sp, slot)
            for r in range(RING):
                sp.wait_ge(stored[r], 16 * len(range(r, CHUNKS, RING)))

        @block.tensor
        def _(pe):
            def project(c, i):
                src, w, loaded = ((xT_s, wq_s, xT_loaded), (cT_s, wk_s, cT_loaded))[i]
                pe.wait_ge(loaded[c.ring], c.ring_times(16, 16))
                if not c.has((4, 2)[i]):
                    if c.has(1):
                        pe.wait_ge(v_placed, c.times(4, (-2, 0)[i]))
                elif i == 0:
                    pe.wait_ge(y_ready, c.times(1, -3))
                else:
                    pe.wait_ge(maxT_ready, c.times(1, -1))
                pe.matmul((misc0, misc1)[i][:, :], w[:, :], src[:, c.ring, :], start=True,
                          stop=True).then_inc(projected[i], 1)

            def project_v(c, half):
                pe.wait_ge(hi_ready[half], c.times(1, 1))
                pe.wait_ge(rest_ready[half], c.times(1, 1))
                for j in range(CB // 2):
                    rows = cT_s[:, c.ring, :].rearrange("p (b s) -> p b s", s=SEQ)[:, half * CB // 2 + j, :]
                    for e in range(2):
                        mm = pe.matmul((misc0, misc1)[half][e * SEQ:(e + 1) * SEQ, j * P:(j + 1) * P],
                                       rows, wv_s[:, :], start=True, stop=True)
                mm.then_inc(v_projected, 1)

            def score_rows(c, u):
                b2, half = u // 2, u % 2
                if u == 0:
                    pe.wait_ge(stack_loaded[c.ring], c.ring_times(STACK_LOADS, STACK_LOADS))
                if u >= 2 or c.has(1):
                    pe.wait_ge(rows_maxed, c.times(UNITS, u - 1))
                for b in range(2):
                    for j in range(HALF):
                        hp, batch = half * HALF + j, 2 * b2 + b
                        mm = pe.matmul(row_banks[u % 2][b * SEQ:(b + 1) * SEQ, j * 2 * SEQ:(j + 1) * 2 * SEQ],
                                       q_stack[c.ring][0:STACK, hp, batch * SEQ:(batch + 1) * SEQ],
                                       k_stack[c.ring][0:STACK, hp, batch, :, :].rearrange("r e s -> r (e s)"),
                                       start=True, stop=True)
                mm.then_inc(rows_scored, 1)

            def turn_max(c):
                if c.next(1).exists():
                    pe.wait_ge(v_placed, c.next(1).times(4, 4))
                pe.wait_ge(max_split, c.times(1, 1))
                for g in range(2):
                    src = max_parts[:, 2 * g:2 * g + 2, :, :, :].rearrange("p b hp e t -> p (b hp e t)")
                    dst = misc1[0:2 * PAIRS * MAX_ROWS, g * 64:(g + 1) * 64].bitcast(BF16)
                    mm = pe.transpose(dst, src, ident_s[:, :])
                mm.then_inc(max_turned, 1)

            def score_keys(c, b):
                if b == 0:
                    pe.wait_ge(max_loaded[c.ring], c.ring_times(16, 16))
                    if not isinstance(c.turn, int) or c.base < RING:
                        pe.wait_ge(ones_loaded, 16 * RING)
                if b >= 2 or c.has(1):
                    pe.wait_ge(exp_done, c.times(CB, b - 1))
                for hp in range(PAIRS):
                    mm = pe.matmul(key_banks[b % 2][:, hp * SEQ:(hp + 1) * SEQ],
                                   k_stack[c.ring][0:FULL, hp, b, :, :].rearrange("r e s -> r (e s)"),
                                   q_stack[c.ring][0:FULL, hp, b * SEQ:(b + 1) * SEQ],
                                   start=True, stop=True)
                mm.then_inc(keys_scored, 1)

            def weigh_v(c, b):
                if b == 0:
                    pe.wait_ge(v_placed, c.times(4, 4))
                    if c.has(1):
                        pe.wait_ge(attn_ready, c.times(1))
                pe.wait_ge(exp_done, c.times(CB, b + 1))
                for odd in range(2):
                    for g in range(PAIRS // 2):
                        hp = 2 * g + odd
                        mm = pe.matmul(pv_bank[32 * g:32 * g + 32, b * SEQ:(b + 1) * SEQ],
                                       v_cols[c.ring][:, b, hp, :], probs[:, hp, b, :],
                                       start=(odd == 0), stop=(odd == 1))
                if b == CB - 1:
                    mm.then_inc(pv_done, 1)

            def sum_keys(c):
                for odd in range(2):
                    for g in range(PAIRS // 2):
                        mm = pe.matmul(den_bank[32 * g:32 * g + 32, :], den_mask_s[:, odd, :],
                                       probs[:, 2 * g + odd, :, :].rearrange("p b s -> p (b s)"),
                                       start=(odd == 0), stop=(odd == 1))
                mm.then_inc(den_done, 1)

            def project_out(c):
                if c.next(3).exists():
                    pe.wait_ge(v_placed, c.next(3).times(4, 2))
                pe.wait_ge(attn_ready, c.times(1, 1))
                for t in range(TILES):
                    mm = pe.matmul(misc0[:, t * P:(t + 1) * P], attnT[:, t * P:(t + 1) * P], wo_s[:, :],
                                   start=True, stop=True)
                mm.then_inc(out_projected, 1)

            pe.wait_ge(consts_loaded, CONSTS)
            pe.matmul(den_bank[:, 0:P], bv_s[:, :], wo_s[:, :], start=True, stop=True).then_inc(bias_product, 1)
            pe.wait_ge(bias_ready, 1)

            def slot(n):
                p, m, a, f = n.next(2), n.next(1), n, n.next(-1)

                if_exists(p, project, 0)
                if_exists(p, project, 1)
                if_exists(m, score_rows, 0)
                if_exists(m, score_rows, 1)
                if_exists(a, score_keys, 0)
                if_exists(p, project_v, 0)
                if_exists(m, score_rows, 2)
                if_exists(a, score_keys, 1)
                if_exists(a, weigh_v, 0)
                if_exists(p, project_v, 1)
                if_exists(m, score_rows, 3)
                if_exists(m, score_rows, 4)
                if_exists(a, score_keys, 2)
                if_exists(a, weigh_v, 1)
                if_exists(m, score_rows, 5)
                if_exists(a, score_keys, 3)
                if_exists(a, weigh_v, 2)
                if_exists(m, score_rows, 6)
                if_exists(m, score_rows, 7)
                if_exists(a, score_keys, 4)
                if_exists(a, weigh_v, 3)
                if_exists(f, project_out)
                if_exists(a, score_keys, 5)
                if_exists(a, weigh_v, 4)
                if_exists(m, turn_max)
                for b in (6, 7):
                    if_exists(a, score_keys, b)
                    if_exists(a, weigh_v, b - 1)
                if_exists(a, weigh_v, 7)
                if_exists(a, sum_keys)

            slots(pe, slot)

        @block.scalar
        def _(act):
            def take_hi(c, i):
                act.wait_ge(projected[i], c.times(1, 1))
                if c.has(1):
                    act.wait_ge(parts_written[i], c.times(16 * PARTS))
                act.activation(parts[i][0][:, :], (misc0, misc1)[i][:, :], ACT.Identity,
                               bias=bqk_s[:, i:i + 1], scale=1.0).then_inc(hi_ready[i], 1)

            def take_mid(c, i):
                act.wait_ge(rest_ready[i], c.times(1, 1))
                act.activation(parts[i][1][:, :], rest[i][:, :], ACT.Copy).then_inc(mid_ready[i], 1)

            def place_v(c, half):
                act.wait_ge(v_projected, c.times(2, half + 1))
                if c.has(RING):
                    act.wait_ge(pv_done, c.times(1, 1 - RING))
                if not isinstance(c.turn, int) or c.base < RING:
                    act.wait_ge(v_zeroed, RING)
                v = v_cols[c.ring]
                for e in range(2):
                    src = (misc0, misc1)[half][e * SEQ:(e + 1) * SEQ, :].rearrange(
                        "p (bg odd e d) -> p bg odd e d", odd=2, e=2, d=HD)[:, :, :, e, :]
                    row = CB * PAIRS * 32
                    dst = bass.AP(v, e * SEQ * row + half * row // 2 + e * HD,
                                  [[row, SEQ], [64, CB * PAIRS // 4], [32 + 16, 2], [1, HD]])
                    act.activation(dst, src, ACT.Copy).then_inc(v_placed, 1)

            def exponentiate(c, b):
                act.wait_ge(keys_scored, c.times(CB, b + 1))
                if b == 0:
                    if c.has(1):
                        act.wait_ge(den_done, c.times(1))
                act.activation(probs[:, :, b, :], key_banks[b % 2][:, :].rearrange("p (hp s) -> p hp s", s=SEQ),
                               ACT.Exp, scale=SCALE).then_inc(exp_done, 1)

            def copy_max(c):
                act.wait_ge(max_turned, c.times(1, 1))
                if c.has(1):
                    act.wait_ge(maxT_written, c.times(16 * CB // 2))
                n = 2 * PAIRS * MAX_ROWS
                act.activation(maxT[0:n, :, :].rearrange("p g x -> p (g x)"), misc1[0:n, 0:P].bitcast(BF16),
                               ACT.Copy).then_inc(maxT_ready, 1)

            def norm(c):
                act.wait_ge(norm_ready, c.times(1, 1))
                if c.has(RING):
                    act.wait_ge(stored[c.ring], c.ring_times(16))
                for t in range(TILES):
                    i = act.activation(o_s[:, c.ring, t, :], x_s[:, c.ring, t, :], ACT.Identity,
                                       bias=shift[:, t:t + 1], scale=rstd[:, t:t + 1])
                i.then_inc(normed, 1)

            act.wait_ge(consts_loaded, CONSTS)

            def slot(n):
                p, m, a, f = n.next(2), n.next(1), n, n.next(-1)

                if_exists(p, take_hi, 0)
                if_exists(p, take_hi, 1)
                if_exists(p, take_mid, 0)
                if_exists(p, take_mid, 1)
                if_exists(a, exponentiate, 0)
                if_exists(p, place_v, 0)
                if_exists(a, exponentiate, 1)
                if_exists(p, place_v, 1)
                for b in range(2, 6):
                    if_exists(a, exponentiate, b)
                if_exists(m, copy_max)
                if_exists(a, exponentiate, 6)
                if_exists(a, exponentiate, 7)
                if_exists(f, norm)

            slots(act, slot)

        @block.vector
        def _(dve):
            def take_rest(c, i):
                dve.wait_ge(hi_ready[i], c.times(1, 1))
                if c.has(1):
                    dve.wait_ge(lo_ready[i], c.times(1))
                dve.scalar_tensor_tensor(out=rest[i][:, :], in0=(misc0, misc1)[i][:, :],
                                         scalar=bqk_s[:, i:i + 1], in1=parts[i][0][:, :],
                                         op0=ALU.add, op1=ALU.subtract).then_inc(rest_ready[i], 1)

            def invert_sums(c, half):
                dve.wait_ge(den_done, c.times(1, 1))
                if c.has(1):
                    dve.wait_ge(attn_ready, c.times(1))
                at = slice(half * T // 2, (half + 1) * T // 2)
                dve.reciprocal(recip[:, at], den_bank[:, at]).then_inc(recip_done, 1)

            def divide(c):
                dve.wait_ge(recip_done, c.times(2, 2))
                dve.wait_ge(pv_done, c.times(1, 1))
                if c.has(1):
                    dve.wait_ge(out_projected, c.times(1))
                dve.tensor_tensor(attnT[:, :], pv_bank[:, :], recip[:, :], ALU.mult).then_inc(attn_ready, 1)

            def max_rows(c, u):
                dve.wait_ge(rows_scored, c.times(UNITS, u + 1))
                if u == 0:
                    if c.has(1):
                        dve.wait_ge(max_split, c.times(1))
                b2, half = u // 2, u % 2
                dve.tensor_reduce(neg_max[:, b2, half * HALF:(half + 1) * HALF, :].rearrange("p hp e -> p (hp e)"),
                                  row_banks[u % 2][:, :].rearrange("p (h s) -> p h s", s=SEQ), AX_X, ALU.max,
                                  negate=True).then_inc(rows_maxed, 1)

            def split_max(c):
                hi, mid, lo = (max_parts[:, :, :, :, t] for t in range(PARTS))
                dve.wait_ge(rows_maxed, c.times(UNITS, UNITS))
                if c.has(1):
                    dve.wait_ge(max_turned, c.times(1))
                dve.tensor_copy(hi, neg_max[:, :, :, :]).then_inc(max_step, 1)
                dve.wait_ge(max_step, c.times(3, 1))
                dve.tensor_tensor(max_rest[:, :, :, :], neg_max[:, :, :, :], hi, ALU.subtract).then_inc(max_step, 1)
                dve.wait_ge(max_step, c.times(3, 2))
                dve.tensor_copy(mid, max_rest[:, :, :, :]).then_inc(max_step, 1)
                dve.wait_ge(max_step, c.times(3, 3))
                dve.tensor_tensor(lo, max_rest[:, :, :, :], mid, ALU.subtract).then_inc(max_split, 1)

            def add_residual(c):
                dve.wait_ge(out_projected, c.times(1, 1))
                dve.wait_ge(x_biased, c.times(1, 1))
                x_now = x_s[:, c.ring, :, :].rearrange("p t d -> p (t d)")
                dve.tensor_tensor(x_now, misc0[:, :], x_now, ALU.add).then_inc(y_ready, 1)

            def moments(c):
                dve.wait_ge(y_ready, c.times(1, 1))
                if c.has(1):
                    dve.wait_ge(norm_ready, c.times(1))
                for t in range(TILES):
                    i = dve.bn_stats(stats[:, t, :], x_s[:, c.ring, t, :])
                i.then_inc(moments_ready, 1)

            dve.memset(k_stack[0][:, :, :, :, :], 0.0).then_inc(stack_zeroed, 1)
            dve.wait_ge(bias_product, 1)
            dve.tensor_tensor(bo_s[:, :], den_bank[:, 0:P], bo_s[:, :], ALU.add).then_inc(bias_ready, 1)

            def slot(n):
                p, m, f = n.next(2), n.next(1), n.next(-1)

                if_exists(f, invert_sums, 0)
                if_exists(p, take_rest, 0)
                if_exists(p, take_rest, 1)
                if_exists(f, invert_sums, 1)
                if_exists(f, divide)
                for u in range(UNITS):
                    if_exists(m, max_rows, u)
                if_exists(m, split_max)
                if_exists(f, add_residual)
                if_exists(f, moments)

            slots(dve, slot)

        @block.gpsimd
        def _(pool):
            def take_lo(c, i):
                pool.wait_ge(mid_ready[i], c.times(1, 1))
                if c.has(1):
                    pool.wait_ge(parts_written[i], c.times(16 * PARTS))
                pool.tensor_tensor(parts[i][2][:, :], rest[i][:, :], parts[i][1][:, :],
                                   ALU.subtract).then_inc(lo_ready[i], 1)

            def add_bias(c):
                pool.wait_ge(x_loaded[c.ring], c.ring_times(16, 16))
                x_now = x_s[:, c.ring, :, :]
                pool.tensor_tensor(x_now, x_now, bo_s[:, :].unsqueeze(1).broadcast_to([P, TILES, P]),
                                   ALU.add).then_inc(x_biased, 1)

            def norm_factors(c):
                steps = 7

                mean0, dev0, mean1, dev1 = (stats[:, :, k] for k in (1, 2, 4, 5))
                pool.wait_ge(moments_ready, c.times(1, 1))
                pool.tensor_tensor(mean_sum[:, :], mean0, mean1, ALU.add).then_inc(norm_step, 1)
                pool.tensor_tensor(mean_diff[:, :], mean0, mean1, ALU.subtract).then_inc(norm_step, 1)
                pool.tensor_tensor(dev_sum[:, :], dev0, dev1, ALU.add).then_inc(norm_step, 1)
                pool.wait_ge(norm_step, c.times(steps, 3))
                pool.tensor_tensor(diff_sq[:, :], mean_diff[:, :], mean_diff[:, :], ALU.mult)
                pool.tensor_scalar(neg_mean[:, :], mean_sum[:, :], -0.5, None, ALU.mult)
                pool.tensor_scalar(scaled_dev[:, :], dev_sum[:, :], 4.0 / P, 4 * EPS, ALU.mult,
                                   ALU.add).then_inc(norm_step, 1)
                pool.wait_ge(norm_step, c.times(steps, 4))
                pool.tensor_tensor(var4[:, :], scaled_dev[:, :], diff_sq[:, :], ALU.add).then_inc(norm_step, 1)
                pool.wait_ge(norm_step, c.times(steps, 5))
                pool.tensor_tensor(var_eps[:, :], var4[:, :], quarter[:, :], ALU.mult).then_inc(norm_step, 1)
                pool.wait_ge(norm_step, c.times(steps, 6))
                if c.has(1):
                    pool.wait_ge(normed, c.times(1))
                pool.tensor_tensor(rstd[:, :], var_eps[:, :], minus_half[:, :], ALU.pow).then_inc(norm_step, 1)
                pool.wait_ge(norm_step, c.times(steps, 7))
                pool.tensor_tensor(shift[:, :], neg_mean[:, :], rstd[:, :], ALU.mult).then_inc(norm_ready, 1)

            def scale_shift(c):
                o_now = o_s[:, c.ring, :, :]
                pool.wait_ge(normed, c.times(1, 1))
                pool.tensor_tensor(o_now, o_now, gamma_s[:, :].unsqueeze(1).broadcast_to([P, TILES, P]),
                                   ALU.mult).then_inc(scaled, 1)
                pool.wait_ge(scaled, c.times(1, 1))
                pool.tensor_tensor(o_now, o_now, beta_s[:, :].unsqueeze(1).broadcast_to([P, TILES, P]),
                                   ALU.add).then_inc(out_ready, 1)

            for r in range(1, RING):
                pool.wait_ge(stack_zeroed, r)
                pool.memset(k_stack[r][:, :, :, :, :], 0.0).then_inc(stack_zeroed, 1)
            for r in range(RING):
                pool.memset(v_cols[r][:, :, :, :], 0.0).then_inc(v_zeroed, 1)
            pool.memset(minus_half[:, :], -0.5).then_inc(half_set, 1)
            pool.memset(quarter[:, :], 0.25).then_inc(half_set, 1)
            pool.wait_ge(half_set, 2)
            pool.wait_ge(bias_ready, 1)
            pool.wait_ge(consts_loaded, CONSTS)

            def slot(n):
                p, f = n.next(2), n.next(-1)

                if_exists(p, take_lo, 0)
                if_exists(p, take_lo, 1)
                if_exists(f, add_bias)
                if_exists(f, norm_factors)
                if_exists(f, scale_shift)

            slots(pool, slot)


STACK_LOADS = 16 * 2 * 2 * len(RUNS)


def kernel(x, ctx_1024, L0_xattn_Wq, L0_xattn_bq, L0_xattn_Wk, L0_xattn_bk, L0_xattn_Wv, L0_xattn_bv,
           L0_xattn_Wo, L0_xattn_bo, L0_xattn_gamma, L0_xattn_beta):
    import ml_dtypes
    import numpy as np
    from concourse import bacc
    from concourse.bass_utils import run_bass_kernel_spmd

    def rows(a):
        return np.ascontiguousarray(np.asarray(a).reshape(BATCHES * SEQ, P))

    def turned(a):
        return np.ascontiguousarray(rows(a).T)

    def by_member(a):
        a = np.asarray(a)
        return np.ascontiguousarray(np.moveaxis(a.reshape(*a.shape[:-1], PAIRS, 2, HD), -2, -3).reshape(a.shape))

    def in_all_rows(a):
        return np.ascontiguousarray(np.broadcast_to(np.asarray(a)[None, :], (P, P)))

    bf16 = ml_dtypes.bfloat16
    den_mask = np.zeros((2, SEQ, 2, 2, 2, HD), np.float32)
    max_ones = np.zeros((2, PARTS, PAIRS, CB, 2, SEQ), bf16)
    for e in range(2):
        for odd in range(2):
            den_mask[e, :, odd, odd, e, :] = 1
        max_ones[e, :, :, :, e, :] = 1

    arrays = {
        "xT": turned(x), "cT": turned(ctx_1024), "x": rows(x),
        "wq": by_member(L0_xattn_Wq), "wk": by_member(L0_xattn_Wk),
        "wv": np.asarray(L0_xattn_Wv), "wo": np.asarray(L0_xattn_Wo),
        "bqk": np.ascontiguousarray(np.stack([by_member(L0_xattn_bq), by_member(L0_xattn_bk)], 1)),
        "bo": in_all_rows(L0_xattn_bo), "bv_cols": np.ascontiguousarray(in_all_rows(L0_xattn_bv).T),
        "gamma": in_all_rows(L0_xattn_gamma), "beta": in_all_rows(L0_xattn_beta),
        "ident": np.eye(P, dtype=bf16), "den_mask": den_mask.reshape(P, 2, 32),
        "max_ones": max_ones.reshape(MAX_ROWS, PAIRS * CB * 2 * SEQ),
    }
    nc = bacc.Bacc("TRN2", target_bir_lowering=False, num_devices=1)
    args = [nc.dram_tensor(f"{n}_dram", a.shape, mybir.dt.from_np(a.dtype), kind="ExternalInput").ap()
            for n, a in arrays.items()]
    out = nc.dram_tensor("out_dram", [BATCHES * SEQ, P], F32, kind="ExternalOutput").ap()
    xattn_program(nc, *args, out)
    r = run_bass_kernel_spmd(nc, [{f"{n}_dram": a for n, a in arrays.items()}], core_ids=[0])
    return r.results[0]["out_dram"].reshape(BATCHES, SEQ, P)
```

```python
from contextlib import ExitStack

import concourse.bass as bass
from concourse import mybir

F32 = mybir.dt.float32
BF16 = mybir.dt.bfloat16
ALU = mybir.AluOpType
ACT = mybir.ActivationFunctionType
AX_X = mybir.AxisListType.X

P = 128
BATCHES = 128
SEQ = 64
HEADS = 16
HD = P // HEADS
PAIRS = HEADS // 2
EPS = 1e-5
SCALE = HD ** -0.5

CB = 8
T = CB * SEQ
CHUNKS = BATCHES // CB
TILES = T // P
RING = 3
AHEAD = 4
PARTS = 3
RUNS = [(0, 3), (3, 2), (5, 1)]
PRODUCTS = 6
PART_ROWS = HD * 2
STACK = PRODUCTS * PART_ROWS
MAX_ROWS = 2 * PARTS
FULL = STACK + MAX_ROWS
UNITS = CB
HALF = PAIRS // 2
INVERSIONS = 4


class Chunk:

    def __init__(self, turn, base):
        self.turn, self.base = turn, base
        self.ring = base % RING

    def next(self, n):
        return Chunk(self.turn, self.base + n)

    def exists(self):
        return not isinstance(self.turn, int) or 0 <= self.base < CHUNKS

    def has(self, back):
        return self.next(-back).exists()

    def times(self, per, plus=0):
        return self.turn * (per * RING) + (per * self.base + plus)

    def ring_times(self, per, plus=0):
        return self.turn * per + (per * (self.base // RING) + plus)


def if_exists(c, do, *args):
    if c.exists():
        do(c, *args)


def slots(eng, slot):
    first = RING
    full = (CHUNKS - AHEAD - first) // RING
    for n in range(-3, first):
        slot(Chunk(0, n))
    with eng.Fori(0, full) as turn:
        for r in range(RING):
            slot(Chunk(turn, first + r))
    for n in range(first + full * RING, CHUNKS + 2):
        slot(Chunk(0, n))


def xattn_program(nc, xT, cT, x, wq, wk, wv, wo, bqk, bo, bv_cols, gamma, beta, ident, den_mask,
                  max_ones, out):
    x_v = x.rearrange("(c t p) d -> p c t d", p=P, t=TILES)
    out_v = out.rearrange("(c t p) d -> p c t d", p=P, t=TILES)

    with ExitStack() as ctx:
        def sb(name, shape, dt=F32):
            return ctx.enter_context(nc.sbuf_tensor(name, shape, dt))

        def bank(name, dt=F32):
            return ctx.enter_context(nc.psum_tensor(name, [P, 512 if dt == F32 else 1024], dt))

        def sem(name):
            return ctx.enter_context(nc.semaphore(name))

        wq_s, wk_s, wv_s, wo_s = (sb(n, [P, P]) for n in ("wq_s", "wk_s", "wv_s", "wo_s"))
        bqk_s = sb("bqk_s", [P, 2])
        bv_s = sb("bv_s", [P, P])
        bo_s = sb("bo_s", [P, P])
        gamma_s = sb("gamma_s", [P, P])
        beta_s = sb("beta_s", [P, P])
        ident_s = sb("ident_s", [P, P], BF16)
        den_mask_s = sb("den_mask_s", [P, 2, 32])
        xT_s = sb("xT_s", [P, RING, T])
        cT_s = sb("cT_s", [P, RING, T])
        x_s = sb("x_s", [P, RING, TILES, P])
        parts = [[sb(f"part{i}{t}", [P, T], BF16) for t in range(PARTS)] for i in range(2)]
        rest = [sb(f"rest{i}", [P, T]) for i in range(2)]
        q_stack = [sb(f"q_stack{r}", [P, PAIRS, T], BF16) for r in range(RING)]
        k_stack = [sb(f"k_stack{r}", [P, PAIRS, CB, 2, SEQ], BF16) for r in range(RING)]
        v_cols = [sb(f"v_cols{r}", [P, 2, CB // 2, PAIRS, 32]) for r in range(RING)]
        probs = sb("probs", [P, PAIRS, CB, SEQ])
        neg_max = sb("neg_max", [P, CB // 2, PAIRS, 2])
        max_rest = sb("max_rest", [P, CB // 2, PAIRS, 2])
        max_parts = sb("max_parts", [P, CB // 2, PAIRS, 2, PARTS], BF16)
        maxT = sb("maxT", [P, 2, P], BF16)
        pv_s = sb("pv_s", [P, T])
        recip = sb("recip", [P, T])
        attnT = sb("attnT", [P, T])
        stats = sb("stats", [P, TILES, 6])
        minus_half, quarter = sb("minus_half", [P, TILES]), sb("quarter", [P, TILES])
        mean_sum = sb("mean_sum", [P, TILES])
        mean_diff = sb("mean_diff", [P, TILES])
        dev_sum = sb("dev_sum", [P, TILES])
        diff_sq = sb("diff_sq", [P, TILES])
        neg_mean = sb("neg_mean", [P, TILES])
        scaled_dev = sb("scaled_dev", [P, TILES])
        var4 = sb("var4", [P, TILES])
        var_eps = sb("var_eps", [P, TILES])
        rstd = sb("rstd", [P, TILES])
        shift = sb("shift", [P, TILES])

        row_banks = [bank(f"row_bank{i}") for i in range(2)]
        key_banks = [bank(f"key_bank{i}") for i in range(2)]
        pv_bank = bank("pv_bank")
        den_bank = bank("den_bank")
        misc0 = bank("misc0")
        misc1 = bank("misc1")

        part_dram = nc.dram_tensor("part_dram", [RING, 2, PARTS, HD, 2, PAIRS, T], BF16, kind="Internal").ap()
        max_dram = nc.dram_tensor("max_dram", [2, PAIRS * MAX_ROWS, 2 * P], BF16, kind="Internal").ap()

        consts_loaded = sem("consts_loaded")
        ones_loaded = sem("ones_loaded")
        stack_zeroed = sem("stack_zeroed")
        v_zeroed = sem("v_zeroed")
        half_set = sem("half_set")
        bias_product = sem("bias_product")
        bias_ready = sem("bias_ready")
        xT_loaded = [sem(f"xT_loaded{r}") for r in range(RING)]
        cT_loaded = [sem(f"cT_loaded{r}") for r in range(RING)]
        x_loaded = [sem(f"x_loaded{r}") for r in range(RING)]
        projected = [sem("q_projected"), sem("k_projected")]
        v_projected = sem("v_projected")
        hi_ready = [sem("q_hi_ready"), sem("k_hi_ready")]
        rest_ready = [sem("q_rest_ready"), sem("k_rest_ready")]
        mid_ready = [sem("q_mid_ready"), sem("k_mid_ready")]
        lo_ready = [sem("q_lo_ready"), sem("k_lo_ready")]
        parts_written = [[sem(f"{x}_{p}_written") for p in ("hi", "mid", "lo")] for x in "qk"]
        stack_loaded = [sem(f"stack_loaded{r}") for r in range(RING)]
        v_placed = sem("v_placed")
        rows_scored = sem("rows_scored")
        rows_maxed = sem("rows_maxed")
        max_step = sem("max_step")
        max_split = sem("max_split")
        max_turned = sem("max_turned")
        maxT_ready = sem("maxT_ready")
        maxT_written = sem("maxT_written")
        max_loaded = [sem(f"max_loaded{r}") for r in range(RING)]
        keys_scored = sem("keys_scored")
        exp_done = sem("exp_done")
        pv_done = sem("pv_done")
        pv_copied = sem("pv_copied")
        den_done = sem("den_done")
        recip_done = sem("recip_done")
        attn_ready = sem("attn_ready")
        out_projected = sem("out_projected")
        x_biased = sem("x_biased")
        y_ready = sem("y_ready")
        moments_ready = sem("moments_ready")
        norm_step = sem("norm_step")
        norm_ready = sem("norm_ready")
        normed = sem("normed")
        scaled = sem("scaled")
        out_ready = sem("out_ready")
        stored = [sem(f"stored{r}") for r in range(RING)]

        const_loads = [(wq_s, wq), (wk_s, wk), (bqk_s, bqk), (wv_s, wv), (ident_s, ident),
                       (wo_s, wo), (bv_s, bv_cols), (bo_s, bo), (gamma_s, gamma), (beta_s, beta)]
        CONSTS = 16 * (len(const_loads) + 1)

        block = ctx.enter_context(nc.Block())

        @block.sync
        def _(sp):
            def load_turned(c):
                if c.has(RING):
                    sp.wait_ge(projected[0], c.times(1, 1 - RING))
                sp.dma_start(xT_s[:, c.ring, :], xT[:, bass.ds(c.times(T), T)]).then_inc(xT_loaded[c.ring], 16)
                if c.has(RING):
                    sp.wait_ge(v_projected, c.times(1, 1 - RING))
                sp.dma_start(cT_s[:, c.ring, :], cT[:, bass.ds(c.times(T), T)]).then_inc(cT_loaded[c.ring], 16)

            def load_x(c):
                if c.has(RING):
                    sp.wait_ge(stored[c.ring], c.ring_times(16))
                sp.dma_start(x_s[:, c.ring, :, :], x_v[:, c.times(1), :, :]).then_inc(x_loaded[c.ring], 16)

            def write_part(c, t, i):
                sp.wait_ge((hi_ready, mid_ready, lo_ready)[t][i], c.times(1, 1))
                at = t if i == 0 else PARTS - 1 - t
                sp.dma_start(part_dram[c.ring, i, at].rearrange("d e hp x -> (e hp) d x"),
                             parts[i][t][:, :]).then_inc(parts_written[i][t], 16)

            def load_run(c, n):
                first = dict((n, first) for first, n in RUNS)[n]
                row, end = first * PART_ROWS, (first + n) * PART_ROWS
                q_rows, k_rows = (part_dram[c.ring, i].rearrange("t d e hp x -> (t d e) (hp x)") for i in range(2))
                sp.wait_ge(parts_written[0][n - 1], c.times(16, 16))
                sp.dma_start(q_stack[c.ring][row:end, :, :].rearrange("r hp x -> r (hp x)"),
                             q_rows[0:n * PART_ROWS, :]).then_inc(stack_loaded[c.ring], 16)
                sp.wait_ge(parts_written[1][n - 1], c.times(16, 16))
                if not isinstance(c.turn, int) or c.base < RING:
                    sp.wait_ge(stack_zeroed, RING)
                for e in range(2):
                    src = k_rows[(PARTS - n) * PART_ROWS + e:PARTS * PART_ROWS:2, :]
                    sp.dma_start(k_stack[c.ring][row + e:end:2, :, :, e, :].rearrange("r hp b s -> r (hp b) s"),
                                 src.rearrange("r (hb s) -> r hb s", s=SEQ)).then_inc(stack_loaded[c.ring], 16)

            def write_max(c):
                sp.wait_ge(maxT_ready, c.times(1, 1))
                sp.dma_start(max_dram.rearrange("w r x -> (w r) x"),
                             maxT[0:2 * PAIRS * MAX_ROWS, :, :].rearrange("r g x -> r (g x)")).then_inc(maxT_written, 16)

            def load_max(c):
                sp.wait_ge(maxT_written, c.times(16, 16))
                for w in range(2):
                    sp.dma_start(q_stack[c.ring][STACK:FULL, :, w * T // 2:(w + 1) * T // 2],
                                 max_dram[w].rearrange("(hp r) x -> r hp x", r=MAX_ROWS)).then_inc(max_loaded[c.ring], 16)

            def store(c):
                sp.wait_ge(out_ready, c.times(1, 1))
                sp.dma_start(out_v[:, c.times(1), :, :], x_s[:, c.ring, :, :]).then_inc(stored[c.ring], 16)

            sp.dma_start(*[a[:] for a in const_loads[0]]).then_inc(consts_loaded, 16)
            load_turned(Chunk(0, 0))
            for dst, src in const_loads[1:]:
                sp.dma_start(dst[:], src[:]).then_inc(consts_loaded, 16)
            sp.dma_start(den_mask_s[:, :, :], den_mask[:]).then_inc(consts_loaded, 16)
            for r in range(RING):
                sp.wait_ge(stack_zeroed, r + 1)
                sp.dma_start(k_stack[r][STACK:FULL, :, :, :, :].rearrange("r hp b e s -> r (hp b e s)"),
                             max_ones[:]).then_inc(ones_loaded, 16)

            def slot(n):
                p, v, m, g = n.next(3), n.next(2), n.next(1), n.next(-2)
                if_exists(v, load_run, 3)
                if_exists(v, load_run, 2)
                if_exists(v, load_run, 1)
                if_exists(n.next(AHEAD), load_turned)
                for t in range(PARTS):
                    if_exists(p, write_part, t, 0)
                    if_exists(p, write_part, t, 1)
                if_exists(n, load_x)
                if_exists(m, write_max)
                if_exists(g, store)
                if_exists(m, load_max)

            slots(sp, slot)
            for r in range(RING):
                sp.wait_ge(stored[r], 16 * len(range(r, CHUNKS, RING)))

        @block.tensor
        def _(pe):
            def project(c, i):
                src, w, loaded = ((xT_s, wq_s, xT_loaded), (cT_s, wk_s, cT_loaded))[i]
                pe.wait_ge(loaded[c.ring], c.ring_times(16, 16))
                if i == 0 and c.has(5):
                    pe.wait_ge(y_ready, c.times(1, -4))
                elif i == 1 and c.has(3):
                    pe.wait_ge(maxT_ready, c.times(1, -2))
                elif i == 1 and c.has(2):
                    pe.wait_ge(v_placed, c.times(4, -4))
                elif c.has(1):
                    pe.wait_ge(hi_ready[i], c.times(1))
                    pe.wait_ge(rest_ready[i], c.times(1))
                pe.matmul((misc0, misc1)[i][:, :], w[:, :], src[:, c.ring, :], start=True,
                          stop=True).then_inc(projected[i], 1)

            def project_v(c):
                if c.next(1).exists():
                    pe.wait_ge(hi_ready[1], c.next(1).times(1, 1))
                    pe.wait_ge(rest_ready[1], c.next(1).times(1, 1))
                else:
                    pe.wait_ge(maxT_ready, c.times(1, -1))
                for t in range(TILES):
                    mm = pe.matmul(misc1[:, t * P:(t + 1) * P], cT_s[:, c.ring, t * P:(t + 1) * P], wv_s[:, :],
                                   start=True, stop=True)
                mm.then_inc(v_projected, 1)

            def score_rows(c, u):
                b2, half = u // 2, u % 2
                if u == 0:
                    pe.wait_ge(stack_loaded[c.ring], c.ring_times(STACK_LOADS, STACK_LOADS))
                if u >= 2 or c.has(1):
                    pe.wait_ge(rows_maxed, c.times(UNITS, u - 1))
                for b in range(2):
                    for j in range(HALF):
                        hp, batch = half * HALF + j, 2 * b2 + b
                        mm = pe.matmul(row_banks[u % 2][b * SEQ:(b + 1) * SEQ, j * 2 * SEQ:(j + 1) * 2 * SEQ],
                                       q_stack[c.ring][0:STACK, hp, batch * SEQ:(batch + 1) * SEQ],
                                       k_stack[c.ring][0:STACK, hp, batch, :, :].rearrange("r e s -> r (e s)"),
                                       start=True, stop=True)
                mm.then_inc(rows_scored, 1)

            def turn_max(c):
                if c.next(1).exists():
                    pe.wait_ge(v_placed, c.next(1).times(4, 4))
                pe.wait_ge(max_split, c.times(1, 1))
                for g in range(2):
                    src = max_parts[:, 2 * g:2 * g + 2, :, :, :].rearrange("p b hp e t -> p (b hp e t)")
                    dst = misc1[0:2 * PAIRS * MAX_ROWS, g * 64:(g + 1) * 64].bitcast(BF16)
                    mm = pe.transpose(dst, src, ident_s[:, :])
                mm.then_inc(max_turned, 1)

            def score_keys(c, b):
                if b == 0:
                    pe.wait_ge(max_loaded[c.ring], c.ring_times(32, 32))
                    if not isinstance(c.turn, int) or c.base < RING:
                        pe.wait_ge(ones_loaded, 16 * RING)
                if b >= 2 or c.has(1):
                    pe.wait_ge(exp_done, c.times(CB, b - 1))
                for hp in range(PAIRS):
                    mm = pe.matmul(key_banks[b % 2][:, hp * SEQ:(hp + 1) * SEQ],
                                   k_stack[c.ring][0:FULL, hp, b, :, :].rearrange("r e s -> r (e s)"),
                                   q_stack[c.ring][0:FULL, hp, b * SEQ:(b + 1) * SEQ],
                                   start=True, stop=True)
                mm.then_inc(keys_scored, 1)

            def weigh_v(c, b):
                if b == 0:
                    pe.wait_ge(v_placed, c.times(4, 4))
                    if c.has(1):
                        pe.wait_ge(pv_copied, c.times(1))
                pe.wait_ge(exp_done, c.times(CB, b + 1))
                for odd in range(2):
                    for g in range(PAIRS // 2):
                        hp = 2 * g + odd
                        mm = pe.matmul(pv_bank[32 * g:32 * g + 32, b * SEQ:(b + 1) * SEQ],
                                       v_cols[c.ring][:, b % 2, b // 2, hp, :], probs[:, hp, b, :],
                                       start=(odd == 0), stop=(odd == 1))
                if b == CB - 1:
                    mm.then_inc(pv_done, 1)

            def sum_keys(c, odd):
                if odd == 0 and c.has(1):
                    pe.wait_ge(recip_done, c.times(INVERSIONS))
                for g in range(PAIRS // 2):
                    mm = pe.matmul(den_bank[32 * g:32 * g + 32, :], den_mask_s[:, odd, :],
                                   probs[:, 2 * g + odd, :, :].rearrange("p b s -> p (b s)"),
                                   start=(odd == 0), stop=(odd == 1))
                if odd == 1:
                    mm.then_inc(den_done, 1)

            def project_out(c):
                if c.next(4).exists():
                    pe.wait_ge(hi_ready[0], c.next(4).times(1, 1))
                    pe.wait_ge(rest_ready[0], c.next(4).times(1, 1))
                pe.wait_ge(attn_ready, c.times(1, 1))
                for t in range(TILES):
                    mm = pe.matmul(misc0[:, t * P:(t + 1) * P], attnT[:, t * P:(t + 1) * P], wo_s[:, :],
                                   start=True, stop=True)
                mm.then_inc(out_projected, 1)

            pe.wait_ge(consts_loaded, CONSTS)
            pe.matmul(den_bank[:, 0:P], bv_s[:, :], wo_s[:, :], start=True, stop=True).then_inc(bias_product, 1)
            pe.wait_ge(bias_ready, 1)

            def slot(n):
                p, v, m, a, f = n.next(3), n.next(2), n.next(1), n, n.next(-1)

                if_exists(m, score_rows, 0)
                if_exists(p, project, 0)
                if_exists(m, score_rows, 1)
                if_exists(p, project, 1)
                if_exists(m, score_rows, 2)
                if_exists(a, score_keys, 0)
                if_exists(a, score_keys, 1)
                if_exists(m, score_rows, 3)
                if_exists(a, weigh_v, 0)
                if_exists(a, score_keys, 2)
                if_exists(v, project_v)
                if_exists(m, score_rows, 4)
                if_exists(a, weigh_v, 1)
                for b in range(3, 6):
                    if_exists(a, score_keys, b)
                    if_exists(m, score_rows, b + 2)
                    if_exists(a, weigh_v, b - 1)
                if_exists(a, score_keys, 6)
                if_exists(a, weigh_v, 5)
                if_exists(a, score_keys, 7)
                if_exists(a, weigh_v, 6)
                if_exists(a, weigh_v, 7)
                if_exists(a, sum_keys, 0)
                if_exists(m, turn_max)
                if_exists(f, project_out)
                if_exists(a, sum_keys, 1)

            slots(pe, slot)

        @block.scalar
        def _(act):
            def take_hi(c, i):
                act.wait_ge(projected[i], c.times(1, 1))
                if c.has(1):
                    act.wait_ge(parts_written[i][0], c.times(16))
                act.activation(parts[i][0][:, :], (misc0, misc1)[i][:, :], ACT.Identity,
                               bias=bqk_s[:, i:i + 1], scale=1.0).then_inc(hi_ready[i], 1)

            def take_mid(c, i):
                act.wait_ge(rest_ready[i], c.times(1, 1))
                if c.has(1):
                    act.wait_ge(parts_written[i][1], c.times(16))
                act.activation(parts[i][1][:, :], rest[i][:, :], ACT.Copy).then_inc(mid_ready[i], 1)

            def place_v(c, odd_batch):
                act.wait_ge(v_projected, c.times(1, 1))
                if c.has(RING):
                    act.wait_ge(pv_done, c.times(1, 1 - RING))
                if not isinstance(c.turn, int) or c.base < RING:
                    act.wait_ge(v_zeroed, RING)
                row = CB * PAIRS * 32
                for e in range(2):
                    src = misc1[odd_batch * SEQ:(odd_batch + 1) * SEQ, :].rearrange(
                        "p (bg odd e d) -> p bg odd e d", odd=2, e=2, d=HD)[:, :, :, e, :]
                    dst = bass.AP(v_cols[c.ring], e * SEQ * row + odd_batch * row // 2 + e * HD,
                                  [[row, SEQ], [64, CB * PAIRS // 4], [32 + 16, 2], [1, HD]])
                    act.activation(dst, src, ACT.Copy).then_inc(v_placed, 1)

            def copy_pv(c):
                act.wait_ge(pv_done, c.times(1, 1))
                if c.has(1):
                    act.wait_ge(attn_ready, c.times(1))
                act.activation(pv_s[:, :], pv_bank[:, :], ACT.Copy).then_inc(pv_copied, 1)

            def exponentiate(c, b):
                act.wait_ge(keys_scored, c.times(CB, b + 1))
                if b == 0:
                    if c.has(1):
                        act.wait_ge(den_done, c.times(1))
                act.activation(probs[:, :, b, :], key_banks[b % 2][:, :].rearrange("p (hp s) -> p hp s", s=SEQ),
                               ACT.Exp, scale=SCALE).then_inc(exp_done, 1)

            def copy_max(c):
                act.wait_ge(max_turned, c.times(1, 1))
                if c.has(1):
                    act.wait_ge(maxT_written, c.times(16))
                n = 2 * PAIRS * MAX_ROWS
                act.activation(maxT[0:n, :, :].rearrange("p g x -> p (g x)"), misc1[0:n, 0:P].bitcast(BF16),
                               ACT.Copy).then_inc(maxT_ready, 1)

            def norm(c, t):
                if t == 0:
                    act.wait_ge(norm_ready, c.times(1, 1))
                i = act.activation(x_s[:, c.ring, t, :], x_s[:, c.ring, t, :], ACT.Identity,
                                   bias=shift[:, t:t + 1], scale=rstd[:, t:t + 1])
                if t == TILES - 1:
                    i.then_inc(normed, 1)

            act.wait_ge(consts_loaded, CONSTS)

            def slot(n):
                p, v, m, a, f, g = n.next(3), n.next(2), n.next(1), n, n.next(-1), n.next(-2)
                if_exists(f, copy_pv)
                if_exists(p, take_hi, 0)
                if_exists(p, take_hi, 1)
                if_exists(p, take_mid, 0)
                if_exists(a, exponentiate, 0)
                if_exists(p, take_mid, 1)
                if_exists(a, exponentiate, 1)
                for b in range(2, 4):
                    if_exists(a, exponentiate, b)
                    if_exists(v, place_v, b - 2)
                for b in range(4, 8):
                    if_exists(a, exponentiate, b)
                    if_exists(g, norm, b - 4)
                if_exists(m, copy_max)

            slots(act, slot)

        @block.vector
        def _(dve):
            def take_rest(c, i):
                dve.wait_ge(hi_ready[i], c.times(1, 1))
                if c.has(1):
                    dve.wait_ge(lo_ready[i], c.times(1))
                dve.scalar_tensor_tensor(out=rest[i][:, :], in0=(misc0, misc1)[i][:, :],
                                         scalar=bqk_s[:, i:i + 1], in1=parts[i][0][:, :],
                                         op0=ALU.add, op1=ALU.subtract).then_inc(rest_ready[i], 1)

            def invert_sums(c, part):
                dve.wait_ge(den_done, c.times(1, 1))
                if c.has(1):
                    dve.wait_ge(attn_ready, c.times(1))
                at = slice(part * T // INVERSIONS, (part + 1) * T // INVERSIONS)
                dve.reciprocal(recip[:, at], den_bank[:, at]).then_inc(recip_done, 1)

            def divide(c):
                dve.wait_ge(recip_done, c.times(INVERSIONS, INVERSIONS))
                dve.wait_ge(pv_copied, c.times(1, 1))
                if c.has(1):
                    dve.wait_ge(out_projected, c.times(1))
                dve.tensor_tensor(attnT[:, :], pv_s[:, :], recip[:, :], ALU.mult).then_inc(attn_ready, 1)

            def max_rows(c, u):
                dve.wait_ge(rows_scored, c.times(UNITS, u + 1))
                if u == 0:
                    if c.has(1):
                        dve.wait_ge(max_split, c.times(1))
                pair, half = u // 2, u % 2
                place = 2 * (pair % 2) + pair // 2
                dve.tensor_reduce(neg_max[:, place, half * HALF:(half + 1) * HALF, :].rearrange("p hp e -> p (hp e)"),
                                  row_banks[u % 2][:, :].rearrange("p (h s) -> p h s", s=SEQ), AX_X, ALU.max,
                                  negate=True).then_inc(rows_maxed, 1)

            def split_max(c):
                hi, mid, lo = (max_parts[:, :, :, :, t] for t in range(PARTS))
                dve.wait_ge(rows_maxed, c.times(UNITS, UNITS))
                if c.has(1):
                    dve.wait_ge(max_turned, c.times(1))
                dve.tensor_copy(hi, neg_max[:, :, :, :]).then_inc(max_step, 1)
                dve.wait_ge(max_step, c.times(3, 1))
                dve.tensor_tensor(max_rest[:, :, :, :], neg_max[:, :, :, :], hi, ALU.subtract).then_inc(max_step, 1)
                dve.wait_ge(max_step, c.times(3, 2))
                dve.tensor_copy(mid, max_rest[:, :, :, :]).then_inc(max_step, 1)
                dve.wait_ge(max_step, c.times(3, 3))
                dve.tensor_tensor(lo, max_rest[:, :, :, :], mid, ALU.subtract).then_inc(max_split, 1)

            def add_residual(c):
                dve.wait_ge(out_projected, c.times(1, 1))
                dve.wait_ge(x_biased, c.times(1, 1))
                x_now = x_s[:, c.ring, :, :].rearrange("p t d -> p (t d)")
                dve.tensor_tensor(x_now, misc0[:, :], x_now, ALU.add).then_inc(y_ready, 1)

            def moments(c):
                dve.wait_ge(y_ready, c.times(1, 1))
                if c.has(1):
                    dve.wait_ge(norm_ready, c.times(1))
                for t in range(TILES):
                    i = dve.bn_stats(stats[:, t, :], x_s[:, c.ring, t, :])
                i.then_inc(moments_ready, 1)

            dve.memset(k_stack[0][:, :, :, :, :], 0.0).then_inc(stack_zeroed, 1)
            dve.wait_ge(bias_product, 1)
            dve.tensor_tensor(bo_s[:, :], den_bank[:, 0:P], bo_s[:, :], ALU.add).then_inc(bias_ready, 1)

            def slot(n):
                p, m, f = n.next(3), n.next(1), n.next(-1)

                if_exists(f, invert_sums, 0)
                if_exists(m, max_rows, 0)
                if_exists(m, max_rows, 1)
                if_exists(p, take_rest, 0)
                if_exists(p, take_rest, 1)
                for u in range(2, UNITS):
                    if_exists(m, max_rows, u)
                    if u in (2, 4, 5):
                        if_exists(f, invert_sums, {2: 1, 4: 2, 5: 3}[u])
                if_exists(m, split_max)
                if_exists(f, divide)
                if_exists(f, add_residual)
                if_exists(f, moments)

            slots(dve, slot)

        @block.gpsimd
        def _(pool):
            def take_lo(c, i):
                pool.wait_ge(mid_ready[i], c.times(1, 1))
                if c.has(1):
                    pool.wait_ge(parts_written[i][2], c.times(16))
                pool.tensor_tensor(parts[i][2][:, :], rest[i][:, :], parts[i][1][:, :],
                                   ALU.subtract).then_inc(lo_ready[i], 1)

            def add_bias(c):
                pool.wait_ge(x_loaded[c.ring], c.ring_times(16, 16))
                x_now = x_s[:, c.ring, :, :]
                pool.tensor_tensor(x_now, x_now, bo_s[:, :].unsqueeze(1).broadcast_to([P, TILES, P]),
                                   ALU.add).then_inc(x_biased, 1)

            def norm_factors(c):
                steps = 7

                mean0, dev0, mean1, dev1 = (stats[:, :, k] for k in (1, 2, 4, 5))
                pool.wait_ge(moments_ready, c.times(1, 1))
                pool.tensor_tensor(mean_sum[:, :], mean0, mean1, ALU.add).then_inc(norm_step, 1)
                pool.tensor_tensor(mean_diff[:, :], mean0, mean1, ALU.subtract).then_inc(norm_step, 1)
                pool.tensor_tensor(dev_sum[:, :], dev0, dev1, ALU.add).then_inc(norm_step, 1)
                pool.wait_ge(norm_step, c.times(steps, 3))
                pool.tensor_tensor(diff_sq[:, :], mean_diff[:, :], mean_diff[:, :], ALU.mult)
                pool.tensor_scalar(neg_mean[:, :], mean_sum[:, :], -0.5, None, ALU.mult)
                pool.tensor_scalar(scaled_dev[:, :], dev_sum[:, :], 4.0 / P, 4 * EPS, ALU.mult,
                                   ALU.add).then_inc(norm_step, 1)
                pool.wait_ge(norm_step, c.times(steps, 4))
                pool.tensor_tensor(var4[:, :], scaled_dev[:, :], diff_sq[:, :], ALU.add).then_inc(norm_step, 1)
                pool.wait_ge(norm_step, c.times(steps, 5))
                pool.tensor_tensor(var_eps[:, :], var4[:, :], quarter[:, :], ALU.mult).then_inc(norm_step, 1)
                pool.wait_ge(norm_step, c.times(steps, 6))
                if c.has(1):
                    pool.wait_ge(normed, c.times(1))
                pool.tensor_tensor(rstd[:, :], var_eps[:, :], minus_half[:, :], ALU.pow).then_inc(norm_step, 1)
                pool.wait_ge(norm_step, c.times(steps, 7))
                pool.tensor_tensor(shift[:, :], neg_mean[:, :], rstd[:, :], ALU.mult).then_inc(norm_ready, 1)

            def scale_shift(c):
                o_now = x_s[:, c.ring, :, :]
                pool.wait_ge(normed, c.times(1, 1))
                pool.tensor_tensor(o_now, o_now, gamma_s[:, :].unsqueeze(1).broadcast_to([P, TILES, P]),
                                   ALU.mult).then_inc(scaled, 1)
                pool.wait_ge(scaled, c.times(1, 1))
                pool.tensor_tensor(o_now, o_now, beta_s[:, :].unsqueeze(1).broadcast_to([P, TILES, P]),
                                   ALU.add).then_inc(out_ready, 1)

            for r in range(1, RING):
                pool.wait_ge(stack_zeroed, r)
                pool.memset(k_stack[r][:, :, :, :, :], 0.0).then_inc(stack_zeroed, 1)
            for r in range(RING):
                pool.memset(v_cols[r][:, :, :, :], 0.0).then_inc(v_zeroed, 1)
            pool.memset(minus_half[:, :], -0.5).then_inc(half_set, 1)
            pool.memset(quarter[:, :], 0.25).then_inc(half_set, 1)
            pool.wait_ge(half_set, 2)
            pool.wait_ge(bias_ready, 1)
            pool.wait_ge(consts_loaded, CONSTS)

            def slot(n):
                p, f, g = n.next(3), n.next(-1), n.next(-2)
                if_exists(g, norm_factors)
                if_exists(p, take_lo, 0)
                if_exists(p, take_lo, 1)
                if_exists(f, add_bias)
                if_exists(g, scale_shift)

            slots(pool, slot)


STACK_LOADS = 16 * 3 * len(RUNS)


def kernel(x, ctx_1024, L0_xattn_Wq, L0_xattn_bq, L0_xattn_Wk, L0_xattn_bk, L0_xattn_Wv, L0_xattn_bv,
           L0_xattn_Wo, L0_xattn_bo, L0_xattn_gamma, L0_xattn_beta):
    import ml_dtypes
    import numpy as np
    from concourse import bacc
    from concourse.bass_utils import run_bass_kernel_spmd

    def rows(a):
        return np.ascontiguousarray(np.asarray(a).reshape(BATCHES * SEQ, P))

    def turned(a):
        return np.ascontiguousarray(rows(a).T)

    def by_member(a):
        a = np.asarray(a)
        return np.ascontiguousarray(np.moveaxis(a.reshape(*a.shape[:-1], PAIRS, 2, HD), -2, -3).reshape(a.shape))

    def in_all_rows(a):
        return np.ascontiguousarray(np.broadcast_to(np.asarray(a)[None, :], (P, P)))

    bf16 = ml_dtypes.bfloat16
    den_mask = np.zeros((2, SEQ, 2, 2, 2, HD), np.float32)
    max_ones = np.zeros((2, PARTS, PAIRS, CB, 2, SEQ), bf16)
    for e in range(2):
        for odd in range(2):
            den_mask[e, :, odd, odd, e, :] = 1
        max_ones[e, :, :, :, e, :] = 1

    arrays = {
        "xT": turned(x), "cT": turned(ctx_1024), "x": rows(x),
        "wq": by_member(L0_xattn_Wq), "wk": by_member(L0_xattn_Wk),
        "wv": np.asarray(L0_xattn_Wv), "wo": np.asarray(L0_xattn_Wo),
        "bqk": np.ascontiguousarray(np.stack([by_member(L0_xattn_bq), by_member(L0_xattn_bk)], 1)),
        "bo": in_all_rows(L0_xattn_bo), "bv_cols": np.ascontiguousarray(in_all_rows(L0_xattn_bv).T),
        "gamma": in_all_rows(L0_xattn_gamma), "beta": in_all_rows(L0_xattn_beta),
        "ident": np.eye(P, dtype=bf16), "den_mask": den_mask.reshape(P, 2, 32),
        "max_ones": max_ones.reshape(MAX_ROWS, PAIRS * CB * 2 * SEQ),
    }
    nc = bacc.Bacc("TRN2", target_bir_lowering=False, num_devices=1)
    args = [nc.dram_tensor(f"{n}_dram", a.shape, mybir.dt.from_np(a.dtype), kind="ExternalInput").ap()
            for n, a in arrays.items()]
    out = nc.dram_tensor("out_dram", [BATCHES * SEQ, P], F32, kind="ExternalOutput").ap()
    xattn_program(nc, *args, out)
    r = run_bass_kernel_spmd(nc, [{f"{n}_dram": a for n, a in arrays.items()}], core_ids=[0])
    return r.results[0]["out_dram"].reshape(BATCHES, SEQ, P)
```

```python
from contextlib import ExitStack

import concourse.bass as bass
from concourse import mybir

F32 = mybir.dt.float32
BF16 = mybir.dt.bfloat16
ALU = mybir.AluOpType
ACT = mybir.ActivationFunctionType
AX_X = mybir.AxisListType.X

P = 128
BATCHES = 128
SEQ = 64
HEADS = 16
HD = P // HEADS
PAIRS = HEADS // 2
EPS = 1e-5
SCALE = HD ** -0.5

CB = 8
T = CB * SEQ
CHUNKS = BATCHES // CB
TILES = T // P
RING = 3
FIRST_SLOT = -3
AHEAD = 4
PARTS = 3
RUNS = [(0, 3), (3, 2), (5, 1)]
PRODUCTS = 6
PART_ROWS = HD * 2
STACK = PRODUCTS * PART_ROWS
MAX_ROWS = 2 * PARTS
FULL = STACK + MAX_ROWS
UNITS = CB
HALF = PAIRS // 2
INVERSIONS = 4


class Chunk:

    def __init__(self, turn, base):
        self.turn, self.base = turn, base
        self.ring = base % RING

    def next(self, n):
        return Chunk(self.turn, self.base + n)

    def exists(self):
        return not isinstance(self.turn, int) or 0 <= self.base < CHUNKS

    def is_slot(self, number):
        return isinstance(self.turn, int) and self.base == number

    def filling(self):
        return isinstance(self.turn, int) and self.base < 0

    def is_final(self):
        return isinstance(self.turn, int) and self.base == CHUNKS - 1

    def has(self, back):
        return self.next(-back).exists()

    def times(self, per, plus=0):
        return self.turn * (per * RING) + (per * self.base + plus)

    def ring_times(self, per, plus=0):
        return self.turn * per + (per * (self.base // RING) + plus)


def if_exists(c, do, *args):
    if c.exists():
        do(c, *args)


def slots(eng, slot):
    first = RING
    full = (CHUNKS - AHEAD - first) // RING
    for n in range(FIRST_SLOT, first):
        slot(Chunk(0, n))
    with eng.Fori(0, full) as turn:
        for r in range(RING):
            slot(Chunk(turn, first + r))
    for n in range(first + full * RING, CHUNKS + 3):
        slot(Chunk(0, n))


def xattn_program(nc, xT, cT, x, qk_consts, consts, ident, max_ones, out):
    x_v = x.rearrange("(c t p) d -> p c t d", p=P, t=TILES)
    out_v = out.rearrange("(c t p) d -> p c t d", p=P, t=TILES)

    with ExitStack() as ctx:
        def sb(name, shape, dt=F32):
            return ctx.enter_context(nc.sbuf_tensor(name, shape, dt))

        def bank(name, dt=F32):
            return ctx.enter_context(nc.psum_tensor(name, [P, 512 if dt == F32 else 1024], dt))

        def sem(name):
            return ctx.enter_context(nc.semaphore(name))

        qk_consts_s = sb("qk_consts_s", [P, 2 * P + 2])
        wq_s, wk_s = qk_consts_s[:, 0:P], qk_consts_s[:, P:2 * P]
        bqk_s = qk_consts_s[:, 2 * P:2 * P + 2]
        consts_s = sb("consts_s", [P, 6 * P + 64])
        wv_s, wo_s, bv_s, bo_s, gamma_s, beta_s = (consts_s[:, i * P:(i + 1) * P] for i in range(6))
        den_mask_s = consts_s[:, 6 * P:6 * P + 64].rearrange("p (odd c) -> p odd c", odd=2)
        ident_s = sb("ident_s", [P, P], BF16)
        xT_s = sb("xT_s", [P, RING, T])
        cT_s = sb("cT_s", [P, RING, T])
        x_s = sb("x_s", [P, RING, TILES, P])
        parts = [[sb(f"part{i}{t}", [P, T], BF16) for t in range(PARTS)] for i in range(2)]
        rest = [sb(f"rest{i}", [P, T]) for i in range(2)]
        q_stack = [sb(f"q_stack{r}", [P, PAIRS, T], BF16) for r in range(RING)]
        k_stack = [sb(f"k_stack{r}", [P, PAIRS, CB, 2, SEQ], BF16) for r in range(RING)]
        v_cols = [sb(f"v_cols{r}", [P, 2, CB // 2, PAIRS, 32]) for r in range(RING)]
        probs = sb("probs", [P, PAIRS, CB, SEQ])
        neg_max = sb("neg_max", [P, CB // 2, PAIRS, 2])
        max_rest = sb("max_rest", [P, CB // 2, PAIRS, 2])
        max_parts = sb("max_parts", [P, CB // 2, PAIRS, 2, PARTS], BF16)
        maxT = sb("maxT", [P, 2, P], BF16)
        pv_s = sb("pv_s", [P, T])
        recip = sb("recip", [P, T])
        attnT = sb("attnT", [P, T])
        stats = sb("stats", [P, TILES, 6])
        minus_half, quarter = sb("minus_half", [P, TILES]), sb("quarter", [P, TILES])
        mean_sum = sb("mean_sum", [P, TILES])
        mean_diff = sb("mean_diff", [P, TILES])
        dev_sum = sb("dev_sum", [P, TILES])
        diff_sq = sb("diff_sq", [P, TILES])
        neg_mean = sb("neg_mean", [P, TILES])
        scaled_dev = sb("scaled_dev", [P, TILES])
        var4 = sb("var4", [P, TILES])
        var_eps = sb("var_eps", [P, TILES])
        rstd = sb("rstd", [P, TILES])
        shift = sb("shift", [P, TILES])

        row_banks = [bank(f"row_bank{i}") for i in range(2)]
        key_banks = [bank(f"key_bank{i}") for i in range(2)]
        pv_bank = bank("pv_bank")
        den_bank = bank("den_bank")
        misc0 = bank("misc0")
        misc1 = bank("misc1")

        part_dram = nc.dram_tensor("part_dram", [RING, 2, PARTS, HD, 2, PAIRS, T], BF16, kind="Internal").ap()
        max_dram = nc.dram_tensor("max_dram", [2, PAIRS * MAX_ROWS, 2 * P], BF16, kind="Internal").ap()

        qk_consts_loaded = sem("qk_consts_loaded")
        consts_loaded = sem("consts_loaded")
        ones_loaded = [sem(f"ones_loaded{r}") for r in range(RING)]
        stack_zeroed = [sem(f"stack_zeroed{r}") for r in range(RING)]
        v_zeroed = sem("v_zeroed")
        half_set = sem("half_set")
        bias_product = sem("bias_product")
        bias_ready = sem("bias_ready")
        xT_loaded = [sem(f"xT_loaded{r}") for r in range(RING)]
        cT_loaded = [sem(f"cT_loaded{r}") for r in range(RING)]
        x_loaded = [sem(f"x_loaded{r}") for r in range(RING)]
        projected = [sem("q_projected"), sem("k_projected")]
        v_projected = sem("v_projected")
        hi_ready = [sem("q_hi_ready"), sem("k_hi_ready")]
        rest_ready = [sem("q_rest_ready"), sem("k_rest_ready")]
        mid_ready = [sem("q_mid_ready"), sem("k_mid_ready")]
        lo_ready = [sem("q_lo_ready"), sem("k_lo_ready")]
        parts_written = [[sem(f"{x}_{p}_written") for p in ("hi", "mid", "lo")] for x in "qk"]
        stack_loaded = [sem(f"stack_loaded{r}") for r in range(RING)]
        v_placed = sem("v_placed")
        rows_scored = sem("rows_scored")
        rows_maxed = sem("rows_maxed")
        max_step = sem("max_step")
        max_split = sem("max_split")
        max_turned = sem("max_turned")
        maxT_ready = sem("maxT_ready")
        maxT_written = sem("maxT_written")
        max_loaded = [sem(f"max_loaded{r}") for r in range(RING)]
        keys_scored = sem("keys_scored")
        exp_done = sem("exp_done")
        pv_done = sem("pv_done")
        pv_copied = sem("pv_copied")
        den_done = sem("den_done")
        recip_done = sem("recip_done")
        attn_ready = sem("attn_ready")
        out_projected = sem("out_projected")
        x_biased = sem("x_biased")
        y_ready = sem("y_ready")
        moments_ready = sem("moments_ready")
        norm_step = sem("norm_step")
        norm_ready = sem("norm_ready")
        normed = sem("normed")
        scaled = sem("scaled")
        out_ready = sem("out_ready")
        stored = [sem(f"stored{r}") for r in range(RING)]

        block = ctx.enter_context(nc.Block())

        @block.sync
        def _(sp):
            def load_turned(c):
                if c.has(RING):
                    sp.wait_ge(projected[0], c.times(1, 1 - RING))
                sp.dma_start(xT_s[:, c.ring, :], xT[:, bass.ds(c.times(T), T)]).then_inc(xT_loaded[c.ring], 16)
                if c.has(RING):
                    sp.wait_ge(v_projected, c.times(1, 1 - RING))
                sp.dma_start(cT_s[:, c.ring, :], cT[:, bass.ds(c.times(T), T)]).then_inc(cT_loaded[c.ring], 16)

            def load_x(c):
                if c.has(RING):
                    sp.wait_ge(stored[c.ring], c.ring_times(16))
                sp.dma_start(x_s[:, c.ring, :, :], x_v[:, c.times(1), :, :]).then_inc(x_loaded[c.ring], 16)

            def write_part(c, t, i):
                sp.wait_ge((hi_ready, mid_ready, lo_ready)[t][i], c.times(1, 1))
                at = t if i == 0 else PARTS - 1 - t
                sp.dma_start(part_dram[c.ring, i, at].rearrange("d e hp x -> (e hp) d x"),
                             parts[i][t][:, :]).then_inc(parts_written[i][t], 16)

            def load_run(c, n):
                first = dict((n, first) for first, n in RUNS)[n]
                row, end = first * PART_ROWS, (first + n) * PART_ROWS
                q_rows, k_rows = (part_dram[c.ring, i].rearrange("t d e hp x -> (t d e) (hp x)") for i in range(2))
                sp.wait_ge(parts_written[0][n - 1], c.times(16, 16))
                sp.dma_start(q_stack[c.ring][row:end, :, :].rearrange("r hp x -> r (hp x)"),
                             q_rows[0:n * PART_ROWS, :]).then_inc(stack_loaded[c.ring], 16)
                sp.wait_ge(parts_written[1][n - 1], c.times(16, 16))
                if n == 1 and not c.has(RING):
                    sp.wait_ge(stack_zeroed[c.ring], 1)
                    sp.dma_start(k_stack[c.ring][STACK:FULL, :, :, :, :].rearrange("r hp b e s -> r (hp b e s)"),
                                 max_ones[:]).then_inc(ones_loaded[c.ring], 16)
                for e in range(2):
                    src = k_rows[(PARTS - n) * PART_ROWS + e:PARTS * PART_ROWS:2, :]
                    sp.dma_start(k_stack[c.ring][row + e:end:2, :, :, e, :].rearrange("r hp b s -> r (hp b) s"),
                                 src.rearrange("r (hb s) -> r hb s", s=SEQ)).then_inc(stack_loaded[c.ring], 16)

            def write_max(c):
                sp.wait_ge(maxT_ready, c.times(1, 1))
                sp.dma_start(max_dram.rearrange("w r x -> (w r) x"),
                             maxT[0:2 * PAIRS * MAX_ROWS, :, :].rearrange("r g x -> r (g x)")).then_inc(maxT_written, 16)

            def load_max(c):
                sp.wait_ge(maxT_written, c.times(16, 16))
                for w in range(2):
                    if w == 1 and c.has(1):
                        sp.wait_ge(keys_scored, c.times(CB))
                    sp.dma_start(q_stack[c.ring][STACK:FULL, :, w * T // 2:(w + 1) * T // 2],
                                 max_dram[w].rearrange("(hp r) x -> r hp x", r=MAX_ROWS)).then_inc(max_loaded[c.ring], 16)

            def store(c):
                sp.wait_ge(out_ready, c.times(1, 1))
                sp.dma_start(out_v[:, c.times(1), :, :], x_s[:, c.ring, :, :]).then_inc(stored[c.ring], 16)

            sp.dma_start(qk_consts_s[:, :], qk_consts[:]).then_inc(qk_consts_loaded, 16)
            load_turned(Chunk(0, 0))
            for c in range(1, RING):
                load_turned(Chunk(0, c))
            sp.dma_start(consts_s[:, :], consts[:]).then_inc(consts_loaded, 16)
            sp.dma_start(ident_s[:, :], ident[:]).then_inc(consts_loaded, 16)

            def slot(n):
                p, v, m = n.next(3), n.next(2), n.next(1)
                if_exists(v, load_run, 1)
                if_exists(v, load_run, 2)
                if_exists(v, load_run, 3)
                if_exists(n.next(-3), store)
                if n.next(AHEAD).has(RING):
                    if_exists(n.next(AHEAD), load_turned)
                for t in range(PARTS):
                    if_exists(p, write_part, t, 0)
                    if_exists(p, write_part, t, 1)
                    if t == 1:
                        if_exists(m, write_max)
                if_exists(n, load_x)
                if_exists(m, load_max)

            slots(sp, slot)
            for r in range(RING):
                sp.wait_ge(stored[r], 16 * len(range(r, CHUNKS, RING)))

        @block.tensor
        def _(pe):
            def project(c, i):
                src, w, loaded = ((xT_s, wq_s, xT_loaded), (cT_s, wk_s, cT_loaded))[i]
                pe.wait_ge(loaded[c.ring], c.ring_times(16, 16))
                if i == 0 and c.has(5):
                    pe.wait_ge(y_ready, c.times(1, -4))
                elif i == 1 and c.has(3):
                    pe.wait_ge(maxT_ready, c.times(1, -2))
                elif i == 1 and c.has(2):
                    pe.wait_ge(v_placed, c.times(4, -4))
                elif c.has(1):
                    pe.wait_ge(hi_ready[i], c.times(1))
                    pe.wait_ge(rest_ready[i], c.times(1))
                pe.matmul((misc0, misc1)[i][:, :], w[:, :], src[:, c.ring, :], start=True,
                          stop=True).then_inc(projected[i], 1)

            def project_v(c):
                if c.next(1).exists():
                    pe.wait_ge(hi_ready[1], c.next(1).times(1, 1))
                    pe.wait_ge(rest_ready[1], c.next(1).times(1, 1))
                else:
                    pe.wait_ge(maxT_ready, c.times(1, -1))
                for t in range(TILES):
                    mm = pe.matmul(misc1[:, t * P:(t + 1) * P], cT_s[:, c.ring, t * P:(t + 1) * P], wv_s[:, :],
                                   start=True, stop=True)
                mm.then_inc(v_projected, 1)

            def score_rows(c, u):
                b2, half = u // 2, u % 2
                if u == 0:
                    pe.wait_ge(stack_loaded[c.ring], c.ring_times(STACK_LOADS, STACK_LOADS))
                if u >= 2 or c.has(1):
                    pe.wait_ge(rows_maxed, c.times(UNITS, u - 1))
                for b in range(2):
                    for j in range(HALF):
                        hp, batch = half * HALF + j, 2 * b2 + b
                        mm = pe.matmul(row_banks[u % 2][b * SEQ:(b + 1) * SEQ, j * 2 * SEQ:(j + 1) * 2 * SEQ],
                                       q_stack[c.ring][0:STACK, hp, batch * SEQ:(batch + 1) * SEQ],
                                       k_stack[c.ring][0:STACK, hp, batch, :, :].rearrange("r e s -> r (e s)"),
                                       start=True, stop=True)
                mm.then_inc(rows_scored, 1)

            def turn_max(c):
                if c.next(1).exists():
                    pe.wait_ge(v_placed, c.next(1).times(4, 4))
                pe.wait_ge(max_split, c.times(1, 1))
                for g in range(2):
                    src = max_parts[:, 2 * g:2 * g + 2, :, :, :].rearrange("p b hp e t -> p (b hp e t)")
                    dst = misc1[0:2 * PAIRS * MAX_ROWS, g * 64:(g + 1) * 64].bitcast(BF16)
                    mm = pe.transpose(dst, src, ident_s[:, :])
                mm.then_inc(max_turned, 1)

            def score_keys(c, b):
                if b == 0:
                    pe.wait_ge(max_loaded[c.ring], c.ring_times(32, 32))
                    if not c.has(RING):
                        pe.wait_ge(ones_loaded[c.ring], 16)
                if b >= 2 or c.has(1):
                    pe.wait_ge(exp_done, c.times(CB, b - 1))
                for hp in range(PAIRS):
                    mm = pe.matmul(key_banks[b % 2][:, hp * SEQ:(hp + 1) * SEQ],
                                   k_stack[c.ring][0:FULL, hp, b, :, :].rearrange("r e s -> r (e s)"),
                                   q_stack[c.ring][0:FULL, hp, b * SEQ:(b + 1) * SEQ],
                                   start=True, stop=True)
                mm.then_inc(keys_scored, 1)

            def weigh_v(c, b):
                if b == 0:
                    pe.wait_ge(v_placed, c.times(4, 4))
                    if c.has(1):
                        pe.wait_ge(pv_copied, c.times(1))
                pe.wait_ge(exp_done, c.times(CB, b + 1))
                for odd in range(2):
                    for g in range(PAIRS // 2):
                        hp = 2 * g + odd
                        mm = pe.matmul(pv_bank[32 * g:32 * g + 32, b * SEQ:(b + 1) * SEQ],
                                       v_cols[c.ring][:, b % 2, b // 2, hp, :], probs[:, hp, b, :],
                                       start=(odd == 0), stop=(odd == 1))
                if b == CB - 1:
                    mm.then_inc(pv_done, 1)

            def sum_keys(c, odd):
                if odd == 0 and c.has(1):
                    pe.wait_ge(recip_done, c.times(INVERSIONS))
                elif odd == 0:
                    pe.wait_ge(bias_ready, 1)
                for g in range(PAIRS // 2):
                    mm = pe.matmul(den_bank[32 * g:32 * g + 32, :], den_mask_s[:, odd, :],
                                   probs[:, 2 * g + odd, :, :].rearrange("p b s -> p (b s)"),
                                   start=(odd == 0), stop=(odd == 1))
                if odd == 1:
                    mm.then_inc(den_done, 1)

            def project_out(c):
                if c.next(4).exists():
                    pe.wait_ge(hi_ready[0], c.next(4).times(1, 1))
                    pe.wait_ge(rest_ready[0], c.next(4).times(1, 1))
                pe.wait_ge(attn_ready, c.times(1, 1))
                for t in range(TILES):
                    mm = pe.matmul(misc0[:, t * P:(t + 1) * P], attnT[:, t * P:(t + 1) * P], wo_s[:, :],
                                   start=True, stop=True)
                mm.then_inc(out_projected, 1)

            def multiply_bias():
                pe.wait_ge(consts_loaded, 32)
                pe.matmul(den_bank[:, 0:P], bv_s[:, :], wo_s[:, :], start=True, stop=True).then_inc(bias_product, 1)

            pe.wait_ge(qk_consts_loaded, 16)

            def slot(n):
                p, v, m, a, f = n.next(3), n.next(2), n.next(1), n, n.next(-1)

                if n.filling():
                    if_exists(p, project, 0)
                    if_exists(p, project, 1)
                    for u in range(UNITS):
                        if_exists(m, score_rows, u)
                        if u == 5:
                            if_exists(v, project_v)
                    if_exists(m, turn_max)
                    if n.is_slot(FIRST_SLOT):
                        multiply_bias()
                    return
                if_exists(m, score_rows, 0)
                if_exists(p, project, 0)
                if_exists(m, score_rows, 1)
                if_exists(p, project, 1)
                if_exists(m, score_rows, 2)
                if_exists(a, score_keys, 0)
                if_exists(m, score_rows, 3)
                if_exists(a, score_keys, 1)
                if_exists(a, weigh_v, 0)
                if_exists(m, score_rows, 4)
                if_exists(a, score_keys, 2)
                if_exists(v, project_v)
                if_exists(m, score_rows, 5)
                if_exists(a, weigh_v, 1)
                for b in range(3, 5):
                    if_exists(a, score_keys, b)
                    if_exists(m, score_rows, b + 3)
                    if_exists(a, weigh_v, b - 1)
                for b in range(5, CB):
                    if_exists(a, score_keys, b)
                    if_exists(a, weigh_v, b - 1)
                if_exists(m, turn_max)
                if_exists(a, weigh_v, CB - 1)
                if_exists(a, sum_keys, 0)
                if_exists(f, project_out)
                if_exists(a, sum_keys, 1)

            slots(pe, slot)

        @block.scalar
        def _(act):
            def take_hi(c, i):
                act.wait_ge(projected[i], c.times(1, 1))
                if c.has(1):
                    act.wait_ge(parts_written[i][0], c.times(16))
                act.activation(parts[i][0][:, :], (misc0, misc1)[i][:, :], ACT.Identity,
                               bias=bqk_s[:, i:i + 1], scale=1.0).then_inc(hi_ready[i], 1)

            def take_mid(c, i):
                act.wait_ge(rest_ready[i], c.times(1, 1))
                if c.has(1):
                    act.wait_ge(parts_written[i][1], c.times(16))
                act.activation(parts[i][1][:, :], rest[i][:, :], ACT.Copy).then_inc(mid_ready[i], 1)

            def place_v(c, odd_batch):
                act.wait_ge(v_projected, c.times(1, 1))
                if c.has(RING):
                    act.wait_ge(pv_done, c.times(1, 1 - RING))
                if not c.has(RING):
                    act.wait_ge(v_zeroed, c.times(1, 1))
                row = CB * PAIRS * 32
                for e in range(2):
                    src = misc1[odd_batch * SEQ:(odd_batch + 1) * SEQ, :].rearrange(
                        "p (bg odd e d) -> p bg odd e d", odd=2, e=2, d=HD)[:, :, :, e, :]
                    dst = bass.AP(v_cols[c.ring], e * SEQ * row + odd_batch * row // 2 + e * HD,
                                  [[row, SEQ], [64, CB * PAIRS // 4], [32 + 16, 2], [1, HD]])
                    act.activation(dst, src, ACT.Copy).then_inc(v_placed, 1)

            def copy_pv(c):
                act.wait_ge(pv_done, c.times(1, 1))
                if c.has(1):
                    act.wait_ge(attn_ready, c.times(1))
                act.activation(pv_s[:, :], pv_bank[:, :], ACT.Copy).then_inc(pv_copied, 1)

            def exponentiate(c, b):
                act.wait_ge(keys_scored, c.times(CB, b + 1))
                if b == 0:
                    if c.has(1):
                        act.wait_ge(den_done, c.times(1))
                act.activation(probs[:, :, b, :], key_banks[b % 2][:, :].rearrange("p (hp s) -> p hp s", s=SEQ),
                               ACT.Exp, scale=SCALE).then_inc(exp_done, 1)

            def copy_max(c):
                act.wait_ge(max_turned, c.times(1, 1))
                if c.has(1):
                    act.wait_ge(maxT_written, c.times(16))
                n = 2 * PAIRS * MAX_ROWS
                act.activation(maxT[0:n, :, :].rearrange("p g x -> p (g x)"), misc1[0:n, 0:P].bitcast(BF16),
                               ACT.Copy).then_inc(maxT_ready, 1)

            def norm(c, t):
                if t == 0:
                    act.wait_ge(norm_ready, c.times(1, 1))
                i = act.activation(x_s[:, c.ring, t, :], x_s[:, c.ring, t, :], ACT.Identity,
                                   bias=shift[:, t:t + 1], scale=rstd[:, t:t + 1])
                if t == TILES - 1:
                    i.then_inc(normed, 1)

            act.wait_ge(qk_consts_loaded, 16)

            def slot(n):
                p, v, m, a, f, g = n.next(3), n.next(2), n.next(1), n, n.next(-1), n.next(-2)
                if_exists(p, take_hi, 0)
                if_exists(p, take_hi, 1)
                if_exists(a, exponentiate, 0)
                if_exists(p, take_mid, 0)
                if_exists(p, take_mid, 1)
                if_exists(a, exponentiate, 1)
                for b in range(2, 4):
                    if_exists(a, exponentiate, b)
                    if_exists(v, place_v, b - 2)
                if_exists(a, exponentiate, 4)
                if_exists(g, norm, 0)
                if_exists(a, exponentiate, 5)
                if_exists(g, norm, 1)
                if_exists(a, exponentiate, 6)
                if_exists(a, exponentiate, 7)
                if_exists(m, copy_max)
                if_exists(a, copy_pv)
                if_exists(g, norm, 2)
                if_exists(g, norm, 3)

            slots(act, slot)

        @block.vector
        def _(dve):
            def take_rest(c, i):
                dve.wait_ge(hi_ready[i], c.times(1, 1))
                if c.has(1):
                    dve.wait_ge(lo_ready[i], c.times(1))
                dve.scalar_tensor_tensor(out=rest[i][:, :], in0=(misc0, misc1)[i][:, :],
                                         scalar=bqk_s[:, i:i + 1], in1=parts[i][0][:, :],
                                         op0=ALU.add, op1=ALU.subtract).then_inc(rest_ready[i], 1)

            def invert_sums(c, part):
                dve.wait_ge(den_done, c.times(1, 1))
                if c.has(1):
                    dve.wait_ge(attn_ready, c.times(1))
                at = slice(part * T // INVERSIONS, (part + 1) * T // INVERSIONS)
                dve.reciprocal(recip[:, at], den_bank[:, at]).then_inc(recip_done, 1)

            def divide(c):
                dve.wait_ge(recip_done, c.times(INVERSIONS, INVERSIONS))
                dve.wait_ge(pv_copied, c.times(1, 1))
                if c.has(1):
                    dve.wait_ge(out_projected, c.times(1))
                dve.tensor_tensor(attnT[:, :], pv_s[:, :], recip[:, :], ALU.mult).then_inc(attn_ready, 1)

            def max_rows(c, u):
                dve.wait_ge(rows_scored, c.times(UNITS, u + 1))
                if u == 0:
                    if c.has(1):
                        dve.wait_ge(max_split, c.times(1))
                pair, half = u // 2, u % 2
                place = 2 * (pair % 2) + pair // 2
                dve.tensor_reduce(neg_max[:, place, half * HALF:(half + 1) * HALF, :].rearrange("p hp e -> p (hp e)"),
                                  row_banks[u % 2][:, :].rearrange("p (h s) -> p h s", s=SEQ), AX_X, ALU.max,
                                  negate=True).then_inc(rows_maxed, 1)

            def split_max(c):
                hi, mid, lo = (max_parts[:, :, :, :, t] for t in range(PARTS))
                dve.wait_ge(rows_maxed, c.times(UNITS, UNITS))
                if c.has(1):
                    dve.wait_ge(max_turned, c.times(1))
                dve.tensor_copy(hi, neg_max[:, :, :, :]).then_inc(max_step, 1)
                dve.wait_ge(max_step, c.times(3, 1))
                dve.tensor_tensor(max_rest[:, :, :, :], neg_max[:, :, :, :], hi, ALU.subtract).then_inc(max_step, 1)
                dve.wait_ge(max_step, c.times(3, 2))
                dve.tensor_copy(mid, max_rest[:, :, :, :]).then_inc(max_step, 1)
                dve.wait_ge(max_step, c.times(3, 3))
                dve.tensor_tensor(lo, max_rest[:, :, :, :], mid, ALU.subtract).then_inc(max_split, 1)

            def add_residual(c):
                dve.wait_ge(out_projected, c.times(1, 1))
                dve.wait_ge(x_biased, c.times(1, 1))
                x_now = x_s[:, c.ring, :, :].rearrange("p t d -> p (t d)")
                dve.tensor_tensor(x_now, misc0[:, :], x_now, ALU.add).then_inc(y_ready, 1)

            def moments(c):
                dve.wait_ge(y_ready, c.times(1, 1))
                if c.has(1):
                    dve.wait_ge(norm_ready, c.times(1))
                for t in range(TILES):
                    i = dve.bn_stats(stats[:, t, :], x_s[:, c.ring, t, :])
                i.then_inc(moments_ready, 1)

            def scale_shift(c):
                o_now = x_s[:, c.ring, :, :]
                dve.wait_ge(normed, c.times(1, 1))
                dve.tensor_tensor(o_now, o_now, gamma_s[:, :].unsqueeze(1).broadcast_to([P, TILES, P]),
                                  ALU.mult).then_inc(scaled, 1)
                dve.wait_ge(scaled, c.times(1, 1))
                dve.tensor_tensor(o_now, o_now, beta_s[:, :].unsqueeze(1).broadcast_to([P, TILES, P]),
                                  ALU.add).then_inc(out_ready, 1)

            def add_bias_product():
                dve.wait_ge(bias_product, 1)
                dve.tensor_tensor(bo_s[:, :], den_bank[:, 0:P], bo_s[:, :], ALU.add).then_inc(bias_ready, 1)

            dve.memset(k_stack[0][:, :, :, :, :], 0.0).then_inc(stack_zeroed[0], 1)

            def slot(n):
                p, m, f, g = n.next(3), n.next(1), n.next(-1), n.next(-2)

                for u in range(UNITS):
                    if_exists(m, max_rows, u)
                    if u in (0, 4, 5):
                        if_exists(f, invert_sums, (0, 4, 5).index(u))
                    if u in (1, 2):
                        if_exists(p, take_rest, u - 1)
                if_exists(m, split_max)
                if_exists(f, invert_sums, 3)
                if_exists(f, divide)
                if_exists(f, add_residual)
                if_exists(f, moments)
                if g.is_final():
                    scale_shift(g)
                if n.is_slot(FIRST_SLOT):
                    add_bias_product()
                if n.is_slot(FIRST_SLOT + 1):
                    dve.memset(k_stack[2][:, :, :, :, :], 0.0).then_inc(stack_zeroed[2], 1)

            slots(dve, slot)

        @block.gpsimd
        def _(pool):
            def take_lo(c, i):
                pool.wait_ge(mid_ready[i], c.times(1, 1))
                if c.has(1):
                    pool.wait_ge(parts_written[i][2], c.times(16))
                pool.tensor_tensor(parts[i][2][:, :], rest[i][:, :], parts[i][1][:, :],
                                   ALU.subtract).then_inc(lo_ready[i], 1)

            def add_bias(c):
                if not c.has(1):
                    pool.wait_ge(bias_ready, 1)
                pool.wait_ge(x_loaded[c.ring], c.ring_times(16, 16))
                x_now = x_s[:, c.ring, :, :]
                pool.tensor_tensor(x_now, x_now, bo_s[:, :].unsqueeze(1).broadcast_to([P, TILES, P]),
                                   ALU.add).then_inc(x_biased, 1)

            def norm_factors(c):
                steps = 7

                mean0, dev0, mean1, dev1 = (stats[:, :, k] for k in (1, 2, 4, 5))
                pool.wait_ge(moments_ready, c.times(1, 1))
                pool.tensor_tensor(mean_sum[:, :], mean0, mean1, ALU.add).then_inc(norm_step, 1)
                pool.tensor_tensor(mean_diff[:, :], mean0, mean1, ALU.subtract).then_inc(norm_step, 1)
                pool.tensor_tensor(dev_sum[:, :], dev0, dev1, ALU.add).then_inc(norm_step, 1)
                pool.wait_ge(norm_step, c.times(steps, 3))
                pool.tensor_tensor(diff_sq[:, :], mean_diff[:, :], mean_diff[:, :], ALU.mult)
                pool.tensor_scalar(neg_mean[:, :], mean_sum[:, :], -0.5, None, ALU.mult)
                pool.tensor_scalar(scaled_dev[:, :], dev_sum[:, :], 4.0 / P, 4 * EPS, ALU.mult,
                                   ALU.add).then_inc(norm_step, 1)
                pool.wait_ge(norm_step, c.times(steps, 4))
                pool.tensor_tensor(var4[:, :], scaled_dev[:, :], diff_sq[:, :], ALU.add).then_inc(norm_step, 1)
                pool.wait_ge(norm_step, c.times(steps, 5))
                pool.tensor_tensor(var_eps[:, :], var4[:, :], quarter[:, :], ALU.mult).then_inc(norm_step, 1)
                pool.wait_ge(norm_step, c.times(steps, 6))
                if c.has(1):
                    pool.wait_ge(normed, c.times(1))
                pool.tensor_tensor(rstd[:, :], var_eps[:, :], minus_half[:, :], ALU.pow).then_inc(norm_step, 1)
                pool.wait_ge(norm_step, c.times(steps, 7))
                pool.tensor_tensor(shift[:, :], neg_mean[:, :], rstd[:, :], ALU.mult).then_inc(norm_ready, 1)

            def scale_shift(c):
                o_now = x_s[:, c.ring, :, :]
                pool.wait_ge(normed, c.times(1, 1))
                pool.tensor_tensor(o_now, o_now, gamma_s[:, :].unsqueeze(1).broadcast_to([P, TILES, P]),
                                   ALU.mult).then_inc(scaled, 1)
                pool.wait_ge(scaled, c.times(1, 1))
                pool.tensor_tensor(o_now, o_now, beta_s[:, :].unsqueeze(1).broadcast_to([P, TILES, P]),
                                   ALU.add).then_inc(out_ready, 1)

            pool.memset(minus_half[:, :], -0.5).then_inc(half_set, 1)
            pool.memset(quarter[:, :], 0.25).then_inc(half_set, 1)
            pool.wait_ge(half_set, 2)
            pool.memset(k_stack[1][:, :, :, :, :], 0.0).then_inc(stack_zeroed[1], 1)
            pool.memset(v_cols[0][:, :, :, :, :], 0.0).then_inc(v_zeroed, 1)

            def slot(n):
                p, f, g = n.next(3), n.next(-1), n.next(-2)
                if_exists(g, norm_factors)
                if_exists(p, take_lo, 0)
                if_exists(p, take_lo, 1)
                if_exists(f, add_bias)
                if not g.is_final():
                    if_exists(g, scale_shift)
                if n.is_slot(FIRST_SLOT):
                    for r in range(1, RING):
                        pool.memset(v_cols[r][:, :, :, :, :], 0.0).then_inc(v_zeroed, 1)

            slots(pool, slot)


STACK_LOADS = 16 * 3 * len(RUNS)


def kernel(x, ctx_1024, L0_xattn_Wq, L0_xattn_bq, L0_xattn_Wk, L0_xattn_bk, L0_xattn_Wv, L0_xattn_bv,
           L0_xattn_Wo, L0_xattn_bo, L0_xattn_gamma, L0_xattn_beta):
    import ml_dtypes
    import numpy as np
    from concourse import bacc
    from concourse.bass_utils import run_bass_kernel_spmd

    def rows(a):
        return np.ascontiguousarray(np.asarray(a).reshape(BATCHES * SEQ, P))

    def turned(a):
        return np.ascontiguousarray(rows(a).T)

    def by_member(a):
        a = np.asarray(a)
        return np.ascontiguousarray(np.moveaxis(a.reshape(*a.shape[:-1], PAIRS, 2, HD), -2, -3).reshape(a.shape))

    def in_all_rows(a):
        return np.ascontiguousarray(np.broadcast_to(np.asarray(a)[None, :], (P, P)))

    bf16 = ml_dtypes.bfloat16
    den_mask = np.zeros((2, SEQ, 2, 2, 2, HD), np.float32)
    max_ones = np.zeros((2, PARTS, PAIRS, CB, 2, SEQ), bf16)
    for e in range(2):
        for odd in range(2):
            den_mask[e, :, odd, odd, e, :] = 1
        max_ones[e, :, :, :, e, :] = 1

    arrays = {
        "xT": turned(x), "cT": turned(ctx_1024), "x": rows(x),
        "qk_consts": np.concatenate([by_member(a) for a in (L0_xattn_Wq, L0_xattn_Wk)]
                                    + [by_member(a)[:, None] for a in (L0_xattn_bq, L0_xattn_bk)], 1),
        "consts": np.concatenate([np.asarray(L0_xattn_Wv), np.asarray(L0_xattn_Wo), in_all_rows(L0_xattn_bv).T,
                                  in_all_rows(L0_xattn_bo), in_all_rows(L0_xattn_gamma),
                                  in_all_rows(L0_xattn_beta), den_mask.reshape(P, 64)], 1),
        "ident": np.eye(P, dtype=bf16),
        "max_ones": max_ones.reshape(MAX_ROWS, PAIRS * CB * 2 * SEQ),
    }
    nc = bacc.Bacc("TRN2", target_bir_lowering=False, num_devices=1)
    args = [nc.dram_tensor(f"{n}_dram", a.shape, mybir.dt.from_np(a.dtype), kind="ExternalInput").ap()
            for n, a in arrays.items()]
    out = nc.dram_tensor("out_dram", [BATCHES * SEQ, P], F32, kind="ExternalOutput").ap()
    xattn_program(nc, *args, out)
    r = run_bass_kernel_spmd(nc, [{f"{n}_dram": a for n, a in arrays.items()}], core_ids=[0])
    return r.results[0]["out_dram"].reshape(BATCHES, SEQ, P)
```
